# Optimizing a Trainium2 kernel written in Bass

```python
import numpy as np
import jax
import jax.numpy as jnp

def _softmax(x, axis=-1):
    return jax.nn.softmax(x, axis=axis)

def _gelu(x):
    return jax.nn.gelu(x, approximate=True)

def _silu(x):
    return jax.nn.silu(x)

def _sigmoid(x):
    return jax.nn.sigmoid(x)

def _layernorm(x, axis=-1, eps=1e-05):
    m = jnp.mean(x, axis=axis, keepdims=True)
    v = jnp.var(x, axis=axis, keepdims=True)
    return (x - m) / jnp.sqrt(v + eps)

def _scatter_add(tgt, idx, src, axis=0):
    return tgt.at[idx].add(src)

def _segment_sum(src, seg, n):
    return jax.ops.segment_sum(src, seg, n)
kernel_name = 'mk_seq_preln_d1_jaxref_r8_8eafc3'

def setup_inputs(seed: int=0):
    np.random.seed(seed)
    _w = jnp.asarray

    def _L0_attn_setup():
        import jax, jax.numpy as jnp
        import numpy as np
        D_MODEL = 128
        D_STATE = 16
        D_CONV = 8
        EXPAND = 1
        D_INNER = EXPAND * D_MODEL
        DT_RANK = (D_MODEL + 15) // 16
        FFN_HID = 4 * D_MODEL

        def _layernorm(x, g, b, eps=1e-05):
            mu = jnp.mean(x, axis=-1, keepdims=True)
            var = jnp.var(x, axis=-1, keepdims=True)
            return (x - mu) * jax.lax.rsqrt(var + eps) * g + b

        def _mamba(x, in_proj_w, conv_w, conv_b, x_proj_w, dt_proj_w, dt_proj_b, A_log, D_param, out_proj_w):
            B, T, _ = x.shape
            xz = jnp.einsum('btd,ed->bte', x, in_proj_w)
            xin, z = jnp.split(xz, 2, axis=-1)
            xp = jnp.pad(xin, ((0, 0), (D_CONV - 1, 0), (0, 0)))
            xc = sum((xp[:, k:k + T, :] * conv_w[:, k] for k in range(D_CONV))) + conv_b
            xc = jax.nn.silu(xc)
            dbl = jnp.einsum('btd,ed->bte', xc, x_proj_w)
            dt = dbl[..., :DT_RANK]
            Bmat = dbl[..., DT_RANK:DT_RANK + D_STATE]
            Cmat = dbl[..., DT_RANK + D_STATE:]
            delta = jax.nn.softplus(jnp.einsum('btr,dr->btd', dt, dt_proj_w) + dt_proj_b)
            A = -jnp.exp(A_log)
            dA = jnp.exp(delta[..., None] * A)
            dBx = delta[..., None] * Bmat[:, :, None, :] * xc[..., None]

            def step(h, inp):
                dA_t, dBx_t, C_t = inp
                h = h * dA_t + dBx_t
                y = jnp.einsum('bdn,bn->bd', h, C_t)
                return (h, y)
            h0 = jnp.zeros((B, D_INNER, D_STATE), x.dtype)
            _, ys = jax.lax.scan(step, h0, (dA.transpose(1, 0, 2, 3), dBx.transpose(1, 0, 2, 3), Cmat.transpose(1, 0, 2)))
            y = ys.transpose(1, 0, 2) + xc * D_param
            y = y * jax.nn.silu(z)
            return jnp.einsum('btd,ed->bte', y, out_proj_w)
        key = jax.random.key(seed)
        ks = jax.random.split(key, 16)
        s = lambda *shape: 0.02
        x = jax.random.normal(ks[0], (2, 512, D_MODEL), dtype=jnp.float32)
        in_proj_w = jax.random.normal(ks[1], (2 * D_INNER, D_MODEL), dtype=jnp.float32) * 0.02
        conv_w = jax.random.normal(ks[2], (D_INNER, D_CONV), dtype=jnp.float32) * 0.1
        conv_b = jnp.zeros((D_INNER,), jnp.float32)
        x_proj_w = jax.random.normal(ks[3], (DT_RANK + 2 * D_STATE, D_INNER), dtype=jnp.float32) * 0.02
        dt_proj_w = jax.random.normal(ks[4], (D_INNER, DT_RANK), dtype=jnp.float32) * 0.02
        dt_proj_b = jax.random.uniform(ks[5], (D_INNER,), jnp.float32, -4.0, -2.0)
        A_log = jnp.log(jnp.tile(jnp.arange(1, D_STATE + 1, dtype=jnp.float32)[None, :], (D_INNER, 1)))
        D_param = jnp.ones((D_INNER,), jnp.float32)
        out_proj_w = jax.random.normal(ks[6], (D_MODEL, D_INNER), dtype=jnp.float32) * 0.02
        ln1_g = jnp.ones((D_MODEL,), jnp.float32)
        ln1_b = jnp.zeros((D_MODEL,), jnp.float32)
        ln2_g = jnp.ones((D_MODEL,), jnp.float32)
        ln2_b = jnp.zeros((D_MODEL,), jnp.float32)
        w1 = jax.random.normal(ks[7], (FFN_HID, D_MODEL), dtype=jnp.float32) * 0.02
        b1 = jnp.zeros((FFN_HID,), jnp.float32)
        w2 = jax.random.normal(ks[8], (D_MODEL, FFN_HID), dtype=jnp.float32) * 0.02
        b2 = jnp.zeros((D_MODEL,), jnp.float32)
        return dict(x=x, in_proj_w=in_proj_w, conv_w=conv_w, conv_b=conv_b, x_proj_w=x_proj_w, dt_proj_w=dt_proj_w, dt_proj_b=dt_proj_b, A_log=A_log, D_param=D_param, out_proj_w=out_proj_w, ln1_g=ln1_g, ln1_b=ln1_b, ln2_g=ln2_g, ln2_b=ln2_b, w1=w1, b1=b1, w2=w2, b2=b2)
    _L0_attn_in = _L0_attn_setup()

    def _L0_ffn_setup():
        import jax, jax.numpy as jnp
        import numpy as np
        EPS = 1e-09
        key = jax.random.key(seed)
        k0, k1, k2, k3 = jax.random.split(key, 4)
        B, S, H, F, E = (4, 256, 128, 256, 8)
        return {'hidden_states': jax.random.normal(k0, (B, S, H), dtype=jnp.float32), 'router_w': jax.random.normal(k1, (H, E), dtype=jnp.float32) * 0.02, 'w1': jax.random.normal(k2, (E, H, F), dtype=jnp.float32) * 0.02, 'w2': jax.random.normal(k3, (E, F, H), dtype=jnp.float32) * 0.02}
    _L0_ffn_in = _L0_ffn_setup()
    _d = {'L0_attn_x': _L0_attn_in['x'], 'L0_attn_in_proj_w': _L0_attn_in['in_proj_w'], 'L0_attn_conv_w': _L0_attn_in['conv_w'], 'L0_attn_conv_b': _L0_attn_in['conv_b'], 'L0_attn_x_proj_w': _L0_attn_in['x_proj_w'], 'L0_attn_dt_proj_w': _L0_attn_in['dt_proj_w'], 'L0_attn_dt_proj_b': _L0_attn_in['dt_proj_b'], 'L0_attn_A_log': _L0_attn_in['A_log'], 'L0_attn_D_param': _L0_attn_in['D_param'], 'L0_attn_out_proj_w': _L0_attn_in['out_proj_w'], 'L0_attn_ln1_g': _L0_attn_in['ln1_g'], 'L0_attn_ln1_b': _L0_attn_in['ln1_b'], 'L0_attn_ln2_g': _L0_attn_in['ln2_g'], 'L0_attn_ln2_b': _L0_attn_in['ln2_b'], 'L0_attn_w1': _L0_attn_in['w1'], 'L0_attn_b1': _L0_attn_in['b1'], 'L0_attn_w2': _L0_attn_in['w2'], 'L0_attn_b2': _L0_attn_in['b2'], 'L0_ffn_router_w': _L0_ffn_in['router_w'], 'L0_ffn_w1': _L0_ffn_in['w1'], 'L0_ffn_w2': _L0_ffn_in['w2']}
    _x0 = _d['L0_attn_x']
    _d['L0_attn_x'] = jax.random.normal(jax.random.fold_in(jax.random.key(seed), 1), (8, 512, 128), dtype=_x0.dtype)
    del _x0
    return _d

def reference(L0_attn_x, L0_attn_in_proj_w, L0_attn_conv_w, L0_attn_conv_b, L0_attn_x_proj_w, L0_attn_dt_proj_w, L0_attn_dt_proj_b, L0_attn_A_log, L0_attn_D_param, L0_attn_out_proj_w, L0_attn_ln1_g, L0_attn_ln1_b, L0_attn_ln2_g, L0_attn_ln2_b, L0_attn_w1, L0_attn_b1, L0_attn_w2, L0_attn_b2, L0_ffn_router_w, L0_ffn_w1, L0_ffn_w2):

    def _L0_attn_ref(x, in_proj_w, conv_w, conv_b, x_proj_w, dt_proj_w, dt_proj_b, A_log, D_param, out_proj_w, ln1_g, ln1_b, ln2_g, ln2_b, w1, b1, w2, b2):
        import jax, jax.numpy as jnp
        import numpy as np
        D_MODEL = 128
        D_STATE = 16
        D_CONV = 8
        EXPAND = 1
        D_INNER = EXPAND * D_MODEL
        DT_RANK = (D_MODEL + 15) // 16
        FFN_HID = 4 * D_MODEL

        def _layernorm(x, g, b, eps=1e-05):
            mu = jnp.mean(x, axis=-1, keepdims=True)
            var = jnp.var(x, axis=-1, keepdims=True)
            return (x - mu) * jax.lax.rsqrt(var + eps) * g + b

        def _mamba(x, in_proj_w, conv_w, conv_b, x_proj_w, dt_proj_w, dt_proj_b, A_log, D_param, out_proj_w):
            B, T, _ = x.shape
            xz = jnp.einsum('btd,ed->bte', x, in_proj_w)
            xin, z = jnp.split(xz, 2, axis=-1)
            xp = jnp.pad(xin, ((0, 0), (D_CONV - 1, 0), (0, 0)))
            xc = sum((xp[:, k:k + T, :] * conv_w[:, k] for k in range(D_CONV))) + conv_b
            xc = jax.nn.silu(xc)
            dbl = jnp.einsum('btd,ed->bte', xc, x_proj_w)
            dt = dbl[..., :DT_RANK]
            Bmat = dbl[..., DT_RANK:DT_RANK + D_STATE]
            Cmat = dbl[..., DT_RANK + D_STATE:]
            delta = jax.nn.softplus(jnp.einsum('btr,dr->btd', dt, dt_proj_w) + dt_proj_b)
            A = -jnp.exp(A_log)
            dA = jnp.exp(delta[..., None] * A)
            dBx = delta[..., None] * Bmat[:, :, None, :] * xc[..., None]

            def step(h, inp):
                dA_t, dBx_t, C_t = inp
                h = h * dA_t + dBx_t
                y = jnp.einsum('bdn,bn->bd', h, C_t)
                return (h, y)
            h0 = jnp.zeros((B, D_INNER, D_STATE), x.dtype)
            _, ys = jax.lax.scan(step, h0, (dA.transpose(1, 0, 2, 3), dBx.transpose(1, 0, 2, 3), Cmat.transpose(1, 0, 2)))
            y = ys.transpose(1, 0, 2) + xc * D_param
            y = y * jax.nn.silu(z)
            return jnp.einsum('btd,ed->bte', y, out_proj_w)
        x = x + _mamba(_layernorm(x, ln1_g, ln1_b), in_proj_w, conv_w, conv_b, x_proj_w, dt_proj_w, dt_proj_b, A_log, D_param, out_proj_w)
        h = _layernorm(x, ln2_g, ln2_b)
        h = jax.nn.relu(jnp.einsum('btd,hd->bth', h, w1) + b1)
        x = x + jnp.einsum('bth,dh->btd', h, w2) + b2
        return x

    def _L0_ffn_ref(hidden_states, router_w, w1, w2):
        import jax, jax.numpy as jnp
        import numpy as np
        EPS = 1e-09
        TOP_K = 2
        orig_shape = hidden_states.shape
        H = orig_shape[-1]
        E = router_w.shape[-1]
        flat = hidden_states.reshape(-1, H)
        T = flat.shape[0]
        gate_logits = flat @ router_w
        gate_probs = jax.nn.softmax(gate_logits, axis=-1)
        topk_w, topk_idx = jax.lax.top_k(gate_probs, TOP_K)
        topk_w = topk_w / jnp.clip(topk_w.sum(-1, keepdims=True), EPS)
        cw = jnp.zeros((T, E), dtype=flat.dtype).at[jnp.arange(T)[:, None], topk_idx].add(topk_w)
        h = jax.nn.silu(jnp.einsum('td,edf->etf', flat, w1))
        y = jnp.einsum('etf,efd->etd', h, w2)
        out = jnp.einsum('etd,te->td', y, cw)
        return out.reshape(orig_shape)
    x = L0_attn_x
    x = x + _L0_attn_ref(_layernorm(x, axis=-1), L0_attn_in_proj_w, L0_attn_conv_w, L0_attn_conv_b, L0_attn_x_proj_w, L0_attn_dt_proj_w, L0_attn_dt_proj_b, L0_attn_A_log, L0_attn_D_param, L0_attn_out_proj_w, L0_attn_ln1_g, L0_attn_ln1_b, L0_attn_ln2_g, L0_attn_ln2_b, L0_attn_w1, L0_attn_b1, L0_attn_w2, L0_attn_b2)
    x = x + _L0_ffn_ref(_layernorm(x, axis=-1), L0_ffn_router_w, L0_ffn_w1, L0_ffn_w2)
    return x

_drawn_inputs = setup_inputs


def setup_inputs(seed=0):
    import zlib

    import numpy as np

    out = dict(_drawn_inputs(seed))
    spreads = {'L0_attn_conv_b': (0.0, 0.8),
     'L0_attn_D_param': (1.0, 0.6),
     'L0_attn_ln1_g': (1.0, 0.6),
     'L0_attn_ln1_b': (0.0, 0.8),
     'L0_attn_ln2_g': (1.0, 0.6),
     'L0_attn_ln2_b': (0.0, 2.0),
     'L0_attn_b1': (0.0, 2.0),
     'L0_attn_b2': (0.0, 0.8)}
    factors = {'L0_attn_in_proj_w': 8.0,
     'L0_attn_conv_w': 8.0,
     'L0_attn_x_proj_w': 8.0,
     'L0_attn_dt_proj_w': 8.0,
     'L0_attn_dt_proj_b': 8.0,
     'L0_attn_A_log': 8.0,
     'L0_attn_out_proj_w': 8.0,
     'L0_ffn_router_w': 39.624,
     'L0_ffn_w1': 34.816,
     'L0_ffn_w2': 34.864,
     'L0_attn_w1': 8.0,
     'L0_attn_w2': 8.0}
    for name, (base, spread) in spreads.items():
        noise = np.random.default_rng([zlib.crc32(name.encode()), seed]).standard_normal(out[name].shape)
        drawn = base * np.exp(spread * noise) if base else spread * noise
        out[name] = jnp.asarray(drawn.astype(out[name].dtype))
    for name, factor in factors.items():
        out[name] = (out[name] * factor).astype(out[name].dtype)
    return out
```

```python
import concourse.bass as bass
from concourse import mybir
from contextlib import ExitStack

FP32 = mybir.dt.float32
BF16 = mybir.dt.bfloat16
ALU = mybir.AluOpType
ACT = mybir.ActivationFunctionType
AX = mybir.AxisListType

NB, T, D = 8, 512, 128
P = 128
NT = T // P
NS = 16
KC = 8
HF = 4
NE, FE = 8, 2
EPS_LN, EPS_TOP = 1e-5, 1e-9
BCP = 96

V_CONVB, V_DTB, V_D, V_G1, V_B1, V_G2, V_B2, V_FB, V_ALOG = 0, 1, 2, 3, 4, 5, 6, 7, 11
NV = V_ALOG + NS

R_DA, R_H, R_LAG = 8, 4, 3

FIRST_ROUND, FULL_FROM, FULL_TO, ROUNDS = -1, 3, NB - 1, NB + 2


def stages(i):
    out = []
    for b in (i + 1, i, i - 1, i - 2):
        if isinstance(b, int) and not 0 <= b < NB:
            b = None
        out.append(b)
    return out


def rounds(engine, body):
    for i in range(FIRST_ROUND, FULL_FROM):
        body(i)
    with engine.Fori(FULL_FROM, FULL_TO) as i:
        body(i)
    for i in range(FULL_TO, ROUNDS):
        body(i)


def mamba_moe(nc, x, vecs, in_wT, conv_rows, xbc_wT, xdt_w, dt_wT, out_wT, w1T, w2T, b2, router_w,
              moe_w1, moe_w2, identity, select, tie_limit, out):
    ctx = ExitStack()
    with ctx:
        def sb(name, shape, dt=FP32):
            return ctx.enter_context(nc.sbuf_tensor(name, shape, dt))

        def sem(name):
            return ctx.enter_context(nc.semaphore(name))

        vec = sb("vec", [P, NV])
        inw = sb("inw", [P, 2 * D])
        convb = sb("convb", [P, KC, D])
        convw = sb("convw", [P, KC, D])
        xbcw = sb("xbcw", [P, BCP])
        xdtw = sb("xdtw", [8, D])
        dtw = sb("dtw", [8, D])
        deltaw = sb("deltaw", [P, D])
        outw = sb("outw", [P, D])
        f1w = sb("f1w", [P, HF * P])
        f2w = sb("f2w", [P, HF, D])
        b2row = sb("b2row", [1, D])
        ones = sb("ones", [1, P])
        rw = sb("rw", [P, NE])
        m1w = sb("m1w", [P, NE, FE * P])
        m2w = sb("m2w", [P, NE, FE, D])
        ident = sb("ident", [P, P])
        sel = sb("sel", [BCP, 2 * NS, P], BF16)
        tie = sb("tie", [P, NE * NE])
        expA = sb("expA", [P, NS])
        negA = sb("negA", [P, NS])
        neghalf = sb("neghalf", [P, NT])

        xs = sb("xs", [P, NB * T])
        xa = sb("xa", [P, 4 * T])
        xc = sb("xc", [P, 4 * T])
        zs = sb("zs", [P, 4 * T])
        delta = sb("delta", [P, 2 * T])
        u = sb("u", [P, 2 * T])
        bc = sb("bc", [BCP, 2 * T], BF16)
        cw = sb("cw", [P, NB * NT * NE])

        stat = [sb(f"stat{k}", [P, NT, 6]) for k in range(4)]
        mv = [sb(f"mv{k}", [P, NT, 2]) for k in range(4)]
        vare = [sb(f"vare{k}", [P, NT]) for k in range(4)]
        rstd = [sb(f"rstd{k}", [P, NT]) for k in range(4)]
        xn1 = sb("xn1", [P, T])
        xnT = sb("xnT", [P, KC - 1 + T])
        resid = sb("resid", [BCP, T])
        midp = sb("midp", [BCP, T], BF16)
        absd = sb("absd", [P, T])
        reld = sb("reld", [P, T])
        expd = sb("expd", [P, T])
        lnd = sb("lnd", [P, T])
        roundd = sb("roundd", [P, T])
        fixd = sb("fixd", [P, T])
        lnfix = sb("lnfix", [P, T])
        dA = sb("dA", [P, R_DA, T])
        dBx = sb("dBx", [P, R_H, T])
        hs = sb("hs", [P, R_H, T])
        cs = sb("cs", [P, R_H, T])
        hC = sb("hC", [P, R_H, T])
        ysk = sb("ysk", [P, T])
        yg = sb("yg", [P, T])
        x1 = sb("x1", [P, T])
        xx = sb("xx", [P, T])
        xn2 = sb("xn2", [P, T])
        x2T = sb("x2T", [P, T])
        hid = sb("hid", [P, HF, T])
        xn3 = sb("xn3", [P, T])
        x3T = sb("x3T", [P, T])
        rmax = sb("rmax", [P, NT])
        rlog = sb("rlog", [P, NT, NE])
        rexp = sb("rexp", [P, NT, NE])
        rsum = sb("rsum", [P, NT])
        rinv = sb("rinv", [P, NT])
        prob = sb("prob", [P, NT, NE])
        pdif = sb("pdif", [P, NT, NE, NE])
        pbef = sb("pbef", [P, NT, NE * NE])
        rank = sb("rank", [P, NT, NE])
        topp = sb("topp", [P, NT, NE])
        tsum = sb("tsum", [P, NT])
        tsafe = sb("tsafe", [P, NT])
        tinv = sb("tinv", [P, NT])
        hm = sb("hm", [P, 2 * FE, T])
        ym = sb("ym", [P, 2, T])

        def bank(name):
            return ctx.enter_context(nc.psum_tensor(name, [P, T], FP32))
        pB = [bank("pB0"), bank("pB1")]
        pC = bank("pC")
        pY = bank("pY")
        pG = bank("pG")
        pH = [bank("pH0"), bank("pH1")]
        pO = bank("pO")

        w_loaded, x0_loaded, xr_loaded, wb_loaded = sem("w_loaded"), sem("x0_loaded"), sem("xr_loaded"), sem("wb_loaded")
        consts_set, expA_done, negA_done, convw_done = sem("consts_set"), sem("expA_done"), sem("negA_done"), sem("convw_done")
        deltaw_mm, deltaw_done = sem("deltaw_mm"), sem("deltaw_done")
        stats_done = [sem(f"stats_done{k}") for k in range(4)]
        mv_done = [sem(f"mv_done{k}") for k in range(4)]
        vare_done = [sem(f"vare_done{k}") for k in range(4)]
        rstd_done = [sem(f"rstd_done{k}") for k in range(4)]
        norm_done = [sem(f"norm_done{k}") for k in range(4)]
        t1_mm, xnT_done, conv_mm, xc_done = sem("t1_mm"), sem("xnT_done"), sem("conv_mm"), sem("xc_done")
        z_mm, zs_done, bc_mm, bchi_done = sem("z_mm"), sem("zs_done"), sem("bc_mm"), sem("bchi_done")
        resid_done, midp_done, bc_done = sem("resid_done"), sem("midp_done"), sem("bc_done")
        delta_mm, delta_read, expd_done, lnd_done = sem("delta_mm"), sem("delta_read"), sem("expd_done"), sem("lnd_done")
        roundd_done, fixd_done, lnfix_done, delta_done, u_done = (
            sem("roundd_done"), sem("fixd_done"), sem("lnfix_done"), sem("delta_done"), sem("u_done"))
        B_mm, C_mm, cs_done, dA_done, dBx_done = sem("B_mm"), sem("C_mm"), sem("cs_done"), sem("dA_done"), sem("dBx_done")
        scan_done, hC_done, ysum_mm = sem("scan_done"), sem("hC_done"), sem("ysum_mm")
        ysk_done, yg_done, out_mm, x1_done, xx_done = sem("ysk_done"), sem("yg_done"), sem("out_mm"), sem("x1_done"), sem("xx_done")
        t2_mm, x2T_done, hid_mm, hid_done, ffn_mm, res_done = (
            sem("t2_mm"), sem("x2T_done"), sem("hid_mm"), sem("hid_done"), sem("ffn_mm"), sem("res_done"))
        t3_mm, x3T_done = sem("t3_mm"), sem("x3T_done")
        router_mm, rlog_done, rexp_done, rchain, cw_done = (
            sem("router_mm"), sem("rlog_done"), sem("rexp_done"), sem("rchain"), sem("cw_done"))
        ehid_mm, silu_done, eout_mm, ym_done, acc_done = (
            sem("ehid_mm"), sem("silu_done"), sem("eout_mm"), sem("ym_done"), sem("acc_done"))
        stored = sem("stored")
        parted = {e.engine: sem(f"parted{k}") for k, e in enumerate((nc.scalar, nc.vector, nc.gpsimd))}

        def of(t, b, n=T):
            places = t.shape[1] // n
            return t[:, bass.ds((b if places == NB else b % places) * n, n)]

        def tok(ap, j):
            return ap[:, j * D:(j + 1) * D]

        def apart(engine):
            engine.sem_inc(parted[engine.engine], 1)

        FRONT_LOADS = 9
        BACK_LOADS = 7
        block = ctx.enter_context(nc.Block())

        xv = x.rearrange("b (j p) d -> p b j d", p=P)
        ov = out.rearrange("b (j p) d -> p b j d", p=P)
        xs4 = xs[:, :].rearrange("p (b j d) -> p b j d", b=NB, j=NT)

        @block.sync
        def _(sp):
            sp.dma_start(xs4[:, 0], xv[:, 0]).then_inc(x0_loaded, 16)
            sp.dma_start(vec[:, :], vecs).then_inc(w_loaded, 16)
            sp.dma_start(ident[:, :], identity).then_inc(w_loaded, 16)
            sp.dma_start(inw[:, :], in_wT).then_inc(w_loaded, 16)
            sp.dma_start(convb[:, :, :], conv_rows.unsqueeze(0).broadcast_to([P, KC, D])).then_inc(w_loaded, 16)
            sp.dma_start(xbcw[:, :], xbc_wT).then_inc(w_loaded, 16)
            sp.dma_start(xdtw[:, :], xdt_w).then_inc(w_loaded, 16)
            sp.dma_start(dtw[:, :], dt_wT).then_inc(w_loaded, 16)
            sp.dma_start(sel[:, :, :], select).then_inc(w_loaded, 16)
            sp.dma_start(tie[:, :], tie_limit).then_inc(w_loaded, 16)
            sp.dma_start(xs4[:, 1:NB], xv[:, 1:NB]).then_inc(xr_loaded, 16)
            sp.dma_start(outw[:, :], out_wT).then_inc(wb_loaded, 16)
            sp.dma_start(f1w[:, :], w1T).then_inc(wb_loaded, 16)
            sp.dma_start(f2w[:, :, :], w2T).then_inc(wb_loaded, 16)
            sp.dma_start(b2row[:, :], b2).then_inc(wb_loaded, 16)
            sp.dma_start(rw[:, :], router_w).then_inc(wb_loaded, 16)
            sp.dma_start(m1w[:, :, :], moe_w1).then_inc(wb_loaded, 16)
            sp.dma_start(m2w[:, :, :, :], moe_w2).then_inc(wb_loaded, 16)
            with sp.Fori(0, NB) as b:
                sp.wait_ge(acc_done, b * NE + NE)
                sp.dma_start(ov[:, bass.ds(b, 1)], xs4[:, bass.ds(b, 1)]).then_inc(stored, 16)
            sp.wait_ge(stored, 16 * NB)

        @block.tensor
        def _(pe):
            turns = [(0, "router", 3, rlog_done, 1, 1), (1, "out", 2, x1_done, 1, 1), (4, "t1", 0, xnT_done, 1, 1),
                     (5, "t2", 2, x2T_done, 1, 1), (5, "conv", 0, xc_done, 1, 1), (6, "h0", 2, hid_done, HF, 1),
                     (7, "h1", 2, hid_done, HF, 2), (7, "z", 0, zs_done, 1, 1), (8, "h2", 2, hid_done, HF, 3),
                     (9, "bc", 0, resid_done, 1, 1), (10, "h3", 2, hid_done, HF, 4), (11, "ffn", 2, res_done, 1, 1),
                     (12, "delta", 0, delta_read, 1, 1), (14, "t3", 2, x3T_done, 1, 1)]

            def wait_bank(i, k):
                for back in range(1, 2 * len(turns)):
                    j = k - back
                    r = i if j >= 0 else i - 1
                    if isinstance(r, int) and r < FIRST_ROUND:
                        return
                    _, _, stage, read, per, nth = turns[j % len(turns)]
                    b = stages(r)[stage]
                    if b is not None:
                        pe.wait_ge(read, b * per + nth)
                        return

            def transpose4(dst, src, done):
                for j in range(NT):
                    last = nc.tensor.transpose(tok(dst, j), tok(src, j), ident[:, :])
                last.then_inc(done, 1)

            pe.wait_ge(w_loaded, 16 * FRONT_LOADS)
            nc.tensor.matmul(pG[:, 0:D], xdtw[:, :], dtw[:, :], start=True, stop=True).then_inc(deltaw_mm, 1)
            pe.wait_ge(deltaw_done, 1)

            def product(name, b):
                if name == "router":
                    pe.wait_ge(x3T_done, b + 1)
                    for j in range(NT):
                        last = nc.tensor.matmul(pG[:, j * NE:(j + 1) * NE], x3T[:, j * P:(j + 1) * P],
                                                rw[:, :], start=True, stop=True)
                    last.then_inc(router_mm, 1)
                elif name == "out":
                    pe.wait_ge(yg_done, b + 1)
                    for j in range(NT):
                        last = nc.tensor.matmul(tok(pG, j), yg[:, j * P:(j + 1) * P], outw[:, :], start=True, stop=True)
                    last.then_inc(out_mm, 1)
                elif name == "t1":
                    pe.wait_ge(norm_done[1], b + 1)
                    transpose4(pG, xn1, t1_mm)
                elif name == "t2":
                    pe.wait_ge(norm_done[2], b + 1)
                    transpose4(pG, xn2, t2_mm)
                elif name == "t3":
                    pe.wait_ge(norm_done[3], b + 1)
                    transpose4(pG, xn3, t3_mm)
                elif name == "conv":
                    pe.wait_ge(xnT_done, b + 1)
                    for k in range(KC):
                        last = nc.tensor.matmul(pG[:, :], convw[:, k, :], xnT[:, k:k + T],
                                                start=(k == 0), stop=(k == KC - 1))
                    last.then_inc(conv_mm, 1)
                elif name == "z":
                    nc.tensor.matmul(pG[:, :], inw[:, D:2 * D], xnT[:, KC - 1:], start=True, stop=True).then_inc(z_mm, 1)
                elif name == "bc":
                    pe.wait_ge(xc_done, b + 1)
                    nc.tensor.matmul(pG[0:BCP, :], xbcw[:, :], of(xc, b), start=True, stop=True).then_inc(bc_mm, 1)
                elif name == "delta":
                    nc.tensor.matmul(pG[:, :], deltaw[:, :], of(xc, b), start=True, stop=True).then_inc(delta_mm, 1)
                elif name == "ffn":
                    pe.wait_ge(hid_done, HF * b + HF)
                    for j in range(NT):
                        for k in range(HF):
                            nc.tensor.matmul(tok(pG, j), hid[:, k, j * P:(j + 1) * P], f2w[:, k, :],
                                             start=(k == 0), stop=False)
                        last = nc.tensor.matmul(tok(pG, j), ones[:, :], b2row[:, :], start=False, stop=True)
                    last.then_inc(ffn_mm, 1)
                else:
                    k = int(name[1])
                    if k == 0:
                        pe.wait_ge(x2T_done, b + 1)
                    nc.tensor.matmul(pG[:, :], f1w[:, k * P:(k + 1) * P], x2T[:, :], start=True, stop=True).then_inc(hid_mm, 1)

            def broadcasts(b, n):
                if n == 0:
                    pe.wait_ge(bc_done, 2 * b + 2)
                if not isinstance(b, int) or NS * b + n >= 2:
                    pe.wait_ge(dBx_done, b * NS + n - 1)
                nc.tensor.matmul(pB[n % 2][:, :], sel[:, n, :], of(bc, b), start=True, stop=True).then_inc(B_mm, 1)
                if not isinstance(b, int) or NS * b + n >= 1:
                    pe.wait_ge(cs_done, b * NS + n)
                nc.tensor.matmul(pC[:, :], sel[:, NS + n, :], of(bc, b), start=True, stop=True).then_inc(C_mm, 1)

            def state_sum(b, n):
                if n == 0 and (not isinstance(b, int) or b >= 1):
                    pe.wait_ge(ysk_done, b)
                pe.wait_ge(hC_done, b * NS + n + 1)
                nc.tensor.matmul(pY[:, :], ident[:, :], hC[:, n % R_H, :],
                                 start=(n == 0), stop=(n == NS - 1)).then_inc(ysum_mm, 1)

            def expert_hidden(b, e):
                for f in range(FE):
                    if not isinstance(b, int) or b * NE + e >= 1:
                        pe.wait_ge(silu_done, b * NE * FE + e * FE + f - 1)
                    nc.tensor.matmul(pH[f][:, :], m1w[:, e, f * P:(f + 1) * P], x3T[:, :],
                                     start=True, stop=True).then_inc(ehid_mm, 1)

            def expert_out(b, e):
                pe.wait_ge(silu_done, b * NE * FE + e * FE + 2)
                if not isinstance(b, int) or b * NE + e >= 1:
                    pe.wait_ge(ym_done, b * NE + e)
                for j in range(NT):
                    for f in range(FE):
                        last = nc.tensor.matmul(tok(pO, j), hm[:, (e % 2) * FE + f, j * P:(j + 1) * P], m2w[:, e, f, :],
                                                start=(f == 0), stop=(f == FE - 1))
                last.then_inc(eout_mm, 1)

            def body(i):
                front, scan, middle, expert = stages(i)
                if isinstance(i, int) and i == 1:
                    pe.wait_ge(wb_loaded, 16 * BACK_LOADS)
                for n in range(NS):
                    if scan is not None:
                        if n == 0:
                            broadcasts(scan, 0)
                        if n + 1 < NS:
                            broadcasts(scan, n + 1)
                    for k, (slot, name, stage, *_) in enumerate(turns):
                        b = stages(i)[stage]
                        if slot == n and b is not None:
                            wait_bank(i, k)
                            product(name, b)
                    if scan is not None and n >= R_LAG:
                        state_sum(scan, n - R_LAG)
                    if expert is not None:
                        if n % 4 == 0:
                            expert_hidden(expert, n // 2)
                        if n % 4 == 2:
                            expert_hidden(expert, n // 2)
                        if n % 4 == 3:
                            expert_out(expert, n // 2 - 1)
                        if n % 4 == 1 and n > 1:
                            expert_out(expert, n // 2 - 1)
                if scan is not None:
                    for n in range(NS - R_LAG, NS):
                        state_sum(scan, n)
                if expert is not None:
                    expert_out(expert, NE - 1)

            rounds(pe, body)

        @block.scalar
        def _(act):
            act.wait_ge(w_loaded, 16 * FRONT_LOADS)
            nc.scalar.activation(expA[:, :], vec[:, V_ALOG:V_ALOG + NS], ACT.Exp).then_inc(expA_done, 1)
            act.wait_ge(deltaw_mm, 1)
            nc.scalar.activation(deltaw[:, :], pG[:, 0:D], ACT.Copy).then_inc(deltaw_done, 1)

            def body(i):
                front, scan, middle, expert = stages(i)
                for n in range(NS):
                    if scan is not None and n % 4 == 0:
                        if n == 0:
                            act.wait_ge(delta_done, scan + 1)
                            if isinstance(i, int) and i == 0:
                                act.wait_ge(negA_done, 1)
                        for m in range(n, n + 4):
                            if not isinstance(scan, int) or NS * scan + m >= R_DA:
                                act.wait_ge(scan_done, scan * NS + m - R_DA + 1)
                            apart(act)
                            nc.scalar.activation(dA[:, m % R_DA, :], of(delta, scan), ACT.Exp,
                                                 scale=negA[:, m:m + 1]).then_inc(dA_done, 1)
                    if scan is not None:
                        act.wait_ge(C_mm, scan * NS + n + 1)
                        if not isinstance(scan, int) or NS * scan + n >= R_H:
                            act.wait_ge(hC_done, scan * NS + n - R_H + 1)
                        nc.scalar.activation(cs[:, n % R_H, :], pC[:, :], ACT.Copy).then_inc(cs_done, 1)
                    if expert is not None and n == 0:
                        act.wait_ge(rlog_done, expert + 1)
                        nc.scalar.activation(rexp[:, :, :], rlog[:, :, :], ACT.Exp).then_inc(rexp_done, 1)
                    if front is not None and n == 4:
                        act.wait_ge(t1_mm, front + 1)
                        if isinstance(i, int) and i == FIRST_ROUND:
                            act.wait_ge(consts_set, 1)
                        if not isinstance(front, int) or front >= 1:
                            act.wait_ge(z_mm, front)
                        nc.scalar.activation(xnT[:, KC - 1:], pG[:, :], ACT.Identity, scale=vec[:, V_G1:V_G1 + 1],
                                             bias=vec[:, V_B1:V_B1 + 1]).then_inc(xnT_done, 1)
                    if middle is not None and n == 5:
                        act.wait_ge(t2_mm, middle + 1)
                        nc.scalar.activation(x2T[:, :], pG[:, :], ACT.Identity, scale=vec[:, V_G2:V_G2 + 1],
                                             bias=vec[:, V_B2:V_B2 + 1]).then_inc(x2T_done, 1)
                    if front is not None and n == 5:
                        act.wait_ge(conv_mm, front + 1)
                        apart(act)
                        nc.scalar.activation(of(xc, front), pG[:, :], ACT.Silu,
                                             bias=vec[:, V_CONVB:V_CONVB + 1]).then_inc(xc_done, 1)
                    if middle is not None and n in (6, 7, 8, 10):
                        k = (6, 7, 8, 10).index(n)
                        act.wait_ge(hid_mm, middle * HF + k + 1)
                        nc.scalar.activation(hid[:, k, :], pG[:, :], ACT.Relu,
                                             bias=vec[:, V_FB + k:V_FB + k + 1]).then_inc(hid_done, 1)
                    if front is not None and n == 7:
                        act.wait_ge(z_mm, front + 1)
                        apart(act)
                        nc.scalar.activation(of(zs, front), pG[:, :], ACT.Silu).then_inc(zs_done, 1)
                    if front is not None and n == 9:
                        act.wait_ge(bc_mm, front + 1)
                        apart(act)
                        nc.scalar.activation(of(bc, front), pG[0:BCP, :], ACT.Copy).then_inc(bchi_done, 1)
                    if front is not None and n == 10:
                        act.wait_ge(resid_done, front + 1)
                        nc.scalar.activation(midp[64:96, :], resid[64:96, :], ACT.Copy).then_inc(midp_done, 1)
                        apart(act)
                        nc.scalar.activation(bc[32:64, bass.ds(front % 2 * T, T)], resid[32:64, :], ACT.Copy).then_inc(bc_done, 1)
                    if front is not None and n == 12:
                        bias = vec[:, V_DTB:V_DTB + 1]
                        act.wait_ge(delta_mm, front + 1)
                        nc.scalar.activation(absd[:, :], pG[:, :], ACT.Abs, bias=bias)
                        nc.scalar.activation(reld[:, :], pG[:, :], ACT.Relu, bias=bias).then_inc(delta_read, 1)
                        act.wait_ge(delta_read, front + 1)
                        nc.scalar.activation(expd[:, :], absd[:, :], ACT.Exp, scale=-1.0).then_inc(expd_done, 1)
                        act.wait_ge(expd_done, front + 1)
                        nc.scalar.activation(lnd[:, :], expd[:, :], ACT.Ln, bias=1.0).then_inc(lnd_done, 1)
                    if middle is not None and n == 14:
                        act.wait_ge(t3_mm, middle + 1)
                        if not isinstance(middle, int) or middle >= 1:
                            act.wait_ge(ehid_mm, middle * NE * FE)
                        nc.scalar.activation(x3T[:, :], pG[:, :], ACT.Copy).then_inc(x3T_done, 1)
                    if expert is not None and n % 2 == 1:
                        e = n // 2
                        for f in range(FE):
                            act.wait_ge(ehid_mm, expert * NE * FE + e * FE + f + 1)
                            if not isinstance(expert, int) or expert * NE + e >= 2:
                                act.wait_ge(eout_mm, expert * NE + e - 1)
                            nc.scalar.activation(hm[:, (e % 2) * FE + f, :], pH[f][:, :], ACT.Silu).then_inc(silu_done, 1)

            rounds(act, body)

        @block.vector
        def _(dve):
            nc.vector.memset(xnT[:, 0:KC - 1], 0.0)
            nc.vector.memset(ones[:, :], 1.0)
            nc.vector.memset(neghalf[:, :], -0.5).then_inc(consts_set, 1)
            dve.wait_ge(expA_done, 1)
            nc.vector.tensor_scalar(negA[:, :], expA[:, :], -1.0, None, ALU.mult).then_inc(negA_done, 1)

            def statistics(k, b, src):
                apart(dve)
                for j in range(NT):
                    last = nc.vector.bn_stats(stat[k][:, j, :], tok(src, j))
                last.then_inc(stats_done[k], 1)
                dve.wait_ge(stats_done[k], b + 1)
                apart(dve)
                for j in range(NT):
                    last = nc.vector.bn_aggr(mv[k][:, j, :], stat[k][:, j, :])
                last.then_inc(mv_done[k], 1)

            def normalise(k, b, dst, src):
                dve.wait_ge(rstd_done[k], b + 1)
                apart(dve)
                for j in range(NT):
                    last = nc.vector.tensor_scalar(tok(dst, j), tok(src, j), mv[k][:, j, 0:1], rstd[k][:, j:j + 1],
                                                   ALU.subtract, ALU.mult)
                last.then_inc(norm_done[k], 1)

            def drive(b, n):
                if n == 0:
                    dve.wait_ge(u_done, b + 1)
                dve.wait_ge(B_mm, b * NS + n + 1)
                if not isinstance(b, int) or NS * b + n >= R_H:
                    dve.wait_ge(scan_done, b * NS + n - R_H + 1)
                nc.vector.tensor_tensor(dBx[:, n % R_H, :], of(u, b), pB[n % 2][:, :], ALU.mult).then_inc(dBx_done, 1)

            def router_head(b):
                dve.wait_ge(router_mm, b + 1)
                logits = pG[:, 0:NT * NE].rearrange("p (j e) -> p j e", j=NT)
                nc.vector.tensor_reduce(rmax[:, :], logits, AX.X, ALU.max).then_inc(rchain, 1)
                dve.wait_ge(rchain, R_CHAIN * b + 1)
                nc.vector.tensor_tensor(rlog[:, :, :], logits, rmax[:, :].unsqueeze(2).broadcast_to([P, NT, NE]),
                                        ALU.subtract).then_inc(rlog_done, 1)

            def router_tail(b):
                count = [1]

                def link(op):
                    count[0] += 1
                    op.then_inc(rchain, 1)
                    dve.wait_ge(rchain, R_CHAIN * b + count[0])

                def over_experts(t):
                    return t[:, :].unsqueeze(2).broadcast_to([P, NT, NE])

                dve.wait_ge(rexp_done, b + 1)
                link(nc.vector.tensor_reduce(rsum[:, :], rexp[:, :, :], AX.X, ALU.add))
                link(nc.vector.reciprocal(rinv[:, :], rsum[:, :]))
                link(nc.vector.tensor_tensor(prob[:, :, :], rexp[:, :, :], over_experts(rinv), ALU.mult))
                link(nc.vector.tensor_tensor(pdif[:, :, :, :], prob[:, :, :].unsqueeze(2).broadcast_to([P, NT, NE, NE]),
                                             prob[:, :, :].unsqueeze(3).broadcast_to([P, NT, NE, NE]), ALU.subtract))
                link(nc.vector.tensor_tensor(pbef[:, :, :], pdif[:, :, :, :].rearrange("p t e j -> p t (e j)"),
                                             tie[:, :].unsqueeze(1).broadcast_to([P, NT, NE * NE]), ALU.is_ge))
                link(nc.vector.tensor_reduce(rank[:, :, :], pbef[:, :, :].rearrange("p t (e j) -> p t e j", e=NE),
                                             AX.X, ALU.add))
                link(nc.vector.scalar_tensor_tensor(out=topp[:, :, :], in0=rank[:, :, :], scalar=2.0, in1=prob[:, :, :],
                                                    op0=ALU.is_lt, op1=ALU.mult))
                link(nc.vector.tensor_reduce(tsum[:, :], topp[:, :, :], AX.X, ALU.add))
                link(nc.vector.tensor_scalar(tsafe[:, :], tsum[:, :], EPS_TOP, None, ALU.max))
                link(nc.vector.reciprocal(tinv[:, :], tsafe[:, :]))
                assert count[0] == R_CHAIN
                nc.vector.tensor_tensor(of(cw, b, NT * NE).rearrange("p (j e) -> p j e", j=NT), topp[:, :, :],
                                        over_experts(tinv), ALU.mult).then_inc(cw_done, 1)

            def weigh(b, e):
                dve.wait_ge(eout_mm, b * NE + e + 1)
                if e == 0:
                    dve.wait_ge(cw_done, b + 1)
                if not isinstance(b, int) or b * NE + e >= 2:
                    dve.wait_ge(acc_done, b * NE + e - 1)
                w = of(cw, b, NT * NE).rearrange("p (j e) -> p j e", j=NT)[:, :, e:e + 1].broadcast_to([P, NT, D])
                nc.vector.tensor_tensor(ym[:, e % 2, :].rearrange("p (j d) -> p j d", j=NT),
                                        pO[:, :].rearrange("p (j d) -> p j d", j=NT), w, ALU.mult).then_inc(ym_done, 1)

            def body(i):
                front, scan, middle, expert = stages(i)
                for n in range(NS):
                    if scan is not None:
                        if n == 0:
                            drive(scan, 0)
                        if n + 1 < NS:
                            drive(scan, n + 1)
                        dve.wait_ge(dBx_done, scan * NS + n + 1)
                        dve.wait_ge(dA_done, scan * NS + n + 1)
                        if not isinstance(scan, int) or NS * scan + n >= R_H:
                            dve.wait_ge(hC_done, scan * NS + n - R_H + 1)
                        nc.vector.tensor_tensor_scan(hs[:, n % R_H, :], dA[:, n % R_DA, :], dBx[:, n % R_H, :], 0.0,
                                                     ALU.mult, ALU.add).then_inc(scan_done, 1)
                    if n == 0 and expert is not None:
                        router_head(expert)
                    if n == 0 and middle is not None:
                        dve.wait_ge(ysum_mm, middle * NS + NS)
                        nc.vector.scalar_tensor_tensor(out=ysk[:, :], in0=of(xc, middle), scalar=vec[:, V_D:V_D + 1],
                                                       in1=pY[:, :], op0=ALU.mult, op1=ALU.add).then_inc(ysk_done, 1)
                    if n == 1:
                        if front is not None:
                            if isinstance(i, int) and i == FIRST_ROUND:
                                dve.wait_ge(x0_loaded, 16)
                            if isinstance(i, int) and i == 0:
                                dve.wait_ge(xr_loaded, 16)
                            statistics(0, front, of(xs, front))
                        if expert is not None:
                            router_tail(expert)
                    if n == 2:
                        if middle is not None:
                            dve.wait_ge(out_mm, middle + 1)
                            if not isinstance(middle, int) or middle >= 1:
                                dve.wait_ge(xx_done, middle)
                            nc.vector.tensor_tensor(x1[:, :], of(xa, middle), pG[:, :], ALU.add).then_inc(x1_done, 1)
                            dve.wait_ge(x1_done, middle + 1)
                            statistics(2, middle, x1)
                        if front is not None:
                            normalise(0, front, of(xa, front), of(xs, front))
                            dve.wait_ge(norm_done[0], front + 1)
                            statistics(1, front, of(xa, front))
                    if n == 3:
                        if middle is not None:
                            if not isinstance(middle, int) or middle >= 1:
                                dve.wait_ge(t2_mm, middle)
                            normalise(2, middle, xn2, x1)
                        if front is not None:
                            if not isinstance(front, int) or front >= 1:
                                dve.wait_ge(t1_mm, front)
                            normalise(1, front, xn1, of(xa, front))
                    if n == 10 and front is not None:
                        dve.wait_ge(bchi_done, front + 1)
                        nc.vector.tensor_tensor(resid[:, :], pG[0:BCP, :], of(bc, front), ALU.subtract).then_inc(resid_done, 1)
                    if n == 11 and front is not None:
                        dve.wait_ge(midp_done, front + 1)
                        nc.vector.tensor_tensor(bc[64:96, bass.ds(front % 2 * T, T)], resid[64:96, :], midp[64:96, :],
                                                ALU.subtract).then_inc(bc_done, 1)
                    if n == 11 and middle is not None:
                        dve.wait_ge(ffn_mm, middle + 1)
                        dve.wait_ge(xx_done, middle + 1)
                        nc.vector.tensor_tensor(of(xs, middle), xx[:, :], pG[:, :], ALU.add).then_inc(res_done, 1)
                        dve.wait_ge(res_done, middle + 1)
                        statistics(3, middle, of(xs, middle))
                    if n == 13:
                        if middle is not None:
                            if not isinstance(middle, int) or middle >= 1:
                                dve.wait_ge(t3_mm, middle)
                            normalise(3, middle, xn3, of(xs, middle))
                        if front is not None:
                            dve.wait_ge(expd_done, front + 1)
                            nc.vector.tensor_scalar(roundd[:, :], expd[:, :], 1.0, -1.0, ALU.add, ALU.add).then_inc(roundd_done, 1)
                    if expert is not None:
                        if n % 4 == 0 and n:
                            weigh(expert, n // 2 - 2)
                        if n % 4 == 2 and n > 2:
                            weigh(expert, n // 2 - 2)
                if expert is not None:
                    weigh(expert, NE - 2)
                    weigh(expert, NE - 1)

            rounds(dve, body)

        @block.gpsimd
        def _(pool):
            pool.wait_ge(w_loaded, 16 * FRONT_LOADS)
            nc.gpsimd.tensor_tensor(convw[:, :, :], inw[:, 0:D].unsqueeze(1).broadcast_to([P, KC, D]), convb[:, :, :],
                                    ALU.mult).then_inc(convw_done, 1)
            pool.wait_ge(consts_set, 1)

            def inverse_deviation(k, b):
                pool.wait_ge(mv_done[k], b + 1)
                apart(pool)
                nc.gpsimd.tensor_scalar(vare[k][:, :], mv[k][:, :, 1], EPS_LN, 1.0, ALU.add, ALU.mult).then_inc(vare_done[k], 1)
                pool.wait_ge(vare_done[k], b + 1)
                nc.gpsimd.tensor_tensor(rstd[k][:, :], vare[k][:, :], neghalf[:, :], ALU.pow).then_inc(rstd_done[k], 1)

            def add_expert(b, e):
                pool.wait_ge(ym_done, b * NE + e + 1)
                if not isinstance(b, int) or b * NE + e >= 1:
                    pool.wait_ge(acc_done, b * NE + e)
                apart(pool)
                nc.gpsimd.tensor_tensor(of(xs, b), of(xs, b), ym[:, e % 2, :], ALU.add).then_inc(acc_done, 1)

            def body(i):
                front, scan, middle, expert = stages(i)
                for n in range(NS):
                    if scan is not None:
                        pool.wait_ge(scan_done, scan * NS + n + 1)
                        pool.wait_ge(cs_done, scan * NS + n + 1)
                        if not isinstance(scan, int) or NS * scan + n >= R_H:
                            pool.wait_ge(ysum_mm, scan * NS + n - R_H + 1)
                        nc.gpsimd.tensor_tensor(hC[:, n % R_H, :], hs[:, n % R_H, :], cs[:, n % R_H, :],
                                                ALU.mult).then_inc(hC_done, 1)
                    if n == 0 and middle is not None:
                        pool.wait_ge(ysk_done, middle + 1)
                        if not isinstance(middle, int) or middle >= 1:
                            pool.wait_ge(out_mm, middle)
                        apart(pool)
                        nc.gpsimd.tensor_tensor(yg[:, :], ysk[:, :], of(zs, middle), ALU.mult).then_inc(yg_done, 1)
                    if n == 1 and front is not None:
                        inverse_deviation(0, front)
                    if n == 2 and middle is not None:
                        inverse_deviation(2, middle)
                    if n == 2 and front is not None:
                        inverse_deviation(1, front)
                    if n == 3 and middle is not None:
                        apart(pool)
                        nc.gpsimd.tensor_tensor(xx[:, :], of(xs, middle), x1[:, :], ALU.add).then_inc(xx_done, 1)
                    if n == 11 and middle is not None:
                        inverse_deviation(3, middle)
                    if n == 13 and front is not None:
                        pool.wait_ge(roundd_done, front + 1)
                        nc.gpsimd.tensor_tensor(fixd[:, :], expd[:, :], roundd[:, :], ALU.subtract).then_inc(fixd_done, 1)
                        pool.wait_ge(fixd_done, front + 1)
                        pool.wait_ge(lnd_done, front + 1)
                        nc.gpsimd.tensor_tensor(lnfix[:, :], lnd[:, :], fixd[:, :], ALU.add).then_inc(lnfix_done, 1)
                        pool.wait_ge(lnfix_done, front + 1)
                        apart(pool)
                        nc.gpsimd.tensor_tensor(of(delta, front), lnfix[:, :], reld[:, :], ALU.add).then_inc(delta_done, 1)
                        pool.wait_ge(delta_done, front + 1)
                        apart(pool)
                        nc.gpsimd.tensor_tensor(of(u, front), of(delta, front), of(xc, front), ALU.mult).then_inc(u_done, 1)
                    if expert is not None:
                        if n % 4 == 0 and n:
                            add_expert(expert, n // 2 - 2)
                        if n % 4 == 2 and n > 2:
                            add_expert(expert, n // 2 - 2)
                if expert is not None:
                    add_expert(expert, NE - 2)
                    add_expert(expert, NE - 1)

            rounds(pool, body)


R_CHAIN = 11


def kernel(**inputs):
    import numpy as np
    import ml_dtypes
    import concourse.bacc as bacc
    from concourse.bass_utils import run_bass_kernel_spmd

    a = {k: np.asarray(v) for k, v in inputs.items()}
    g = lambda name: a["L0_attn_" + name]
    columns = [g("conv_b"), g("dt_proj_b"), g("D_param"), g("ln1_g"), g("ln1_b"), g("ln2_g"), g("ln2_b")]
    columns += list(g("b1").reshape(HF, P))
    xp = g("x_proj_w")
    arrays = dict(
        x=g("x"),
        vecs=np.concatenate([np.stack(columns, axis=1), g("A_log")], axis=1),
        in_wT=g("in_proj_w").T,
        conv_rows=g("conv_w").T,
        xbc_wT=np.concatenate([xp[8:40]] * 3, axis=0).T,
        xdt_w=xp[0:8],
        dt_wT=g("dt_proj_w").T,
        out_wT=g("out_proj_w").T,
        w1T=g("w1").T,
        w2T=g("w2").T.reshape(HF, P, D).transpose(1, 0, 2),
        b2=g("b2").reshape(1, D),
        router_w=a["L0_ffn_router_w"],
        moe_w1=a["L0_ffn_w1"].transpose(1, 0, 2),
        moe_w2=a["L0_ffn_w2"].reshape(NE, FE, P, D).transpose(2, 0, 1, 3),
        identity=np.eye(P, dtype=np.float32),
        select=np.broadcast_to((np.arange(BCP)[:, None] % 32 == np.arange(32)[None, :])[:, :, None],
                               (BCP, 32, P)).astype(ml_dtypes.bfloat16),
        tie_limit=np.broadcast_to(np.where(np.arange(NE)[None, :] < np.arange(NE)[:, None], np.float32(0),
                                           np.finfo(np.float32).tiny).reshape(1, NE * NE), (P, NE * NE)),
    )
    arrays = {k: np.ascontiguousarray(v) for k, v in arrays.items()}
    nc = bacc.Bacc("TRN2", target_bir_lowering=False, num_devices=1)
    args = [nc.dram_tensor(f"in_{k}", v.shape, mybir.dt.from_np(v.dtype), kind="ExternalInput").ap()
            for k, v in arrays.items()]
    out = nc.dram_tensor("out_0", (NB, T, D), FP32, kind="ExternalOutput").ap()
    mamba_moe(nc, *args, out)
    r = run_bass_kernel_spmd(nc, [{f"in_{k}": v for k, v in arrays.items()}], core_ids=[0])
    return r.results[0]["out_0"]
```

```python
import concourse.bass as bass
from concourse import mybir
from contextlib import ExitStack

FP32 = mybir.dt.float32
FP32R = mybir.dt.float32r
BF16 = mybir.dt.bfloat16
ALU = mybir.AluOpType
ACT = mybir.ActivationFunctionType
AX = mybir.AxisListType

NB, T, D = 8, 512, 128
P = 128
NT = T // P
NS = 16
KC = 8
HF = 4
NE, FE = 8, 2
EPS_LN, EPS_TOP = 1e-5, 1e-9
HALF_ROOT = 0.5 ** 0.5
BCP = 96

V_CONVB, V_DTB, V_D, V_G1, V_B1, V_G2, V_B2, V_FB, V_ALOG = 0, 1, 2, 3, 4, 5, 6, 7, 11
NV = V_ALOG + NS

R_H, R_HC = 4, 8
P_DA = 12

FIRST_ROUND, FULL_FROM, FULL_TO, ROUNDS = -2, 4, NB - 2, NB + 3


NORMS, FRONT, SCAN, MIDDLE, EXPERT, TAIL = range(6)


def stages(i):
    out = []
    for b in (i + 2, i + 1, i, i - 1, i - 2, i - 3):
        if isinstance(b, int) and not 0 <= b < NB:
            b = None
        out.append(b)
    return out


def rounds(engine, body):
    for i in range(FIRST_ROUND, FULL_FROM):
        body(i)
    with engine.Fori(FULL_FROM, FULL_TO) as i:
        body(i)
    for i in range(FULL_TO, ROUNDS):
        body(i)


def mamba_moe(nc, x, vecs, in_wT, conv_rows, xbc_wT, xdt_w, dt_wT, out_wT, w1T, w2T, b2, router_w,
              moe_w1, moe_w2, identity, select, tie_limit, out):
    ctx = ExitStack()
    with ctx:
        def sb(name, shape, dt=FP32):
            return ctx.enter_context(nc.sbuf_tensor(name, shape, dt))

        def sem(name):
            return ctx.enter_context(nc.semaphore(name))

        vec = sb("vec", [P, NV])
        inw = sb("inw", [P, 2 * D])
        convw = sb("convw", [P, KC, D])
        xbcw = sb("xbcw", [P, BCP])
        xdtw = sb("xdtw", [8, D])
        dtw = sb("dtw", [8, D])
        deltaw = sb("deltaw", [P, D])
        outw = sb("outw", [P, D])
        f1w = sb("f1w", [P, HF * P])
        f2w = sb("f2w", [P, HF, D])
        b2row = sb("b2row", [1, D])
        ones = sb("ones", [1, P])
        rw = sb("rw", [P, NE])
        rwp = [sb(f"rwp{k}", [P, NE], FP32R) for k in range(2)]
        m1wp = [sb(f"m1wp{k}", [P, NE, FE * P], FP32R) for k in range(2)]
        m2w = sb("m2w", [P, NE, FE, D])
        ident = sb("ident", [P, P])
        sel = sb("sel", [BCP, 2 * NS], BF16)
        tie = sb("tie", [P, NE * NE])
        expA = sb("expA", [P, NS])
        negA = sb("negA", [P, NS])
        neghalf = sb("neghalf", [P, NT])

        xs = sb("xs", [P, NB * T])
        xa = sb("xa", [P, 4 * T])
        xc = sb("xc", [P, 2 * T])
        zs = sb("zs", [P, 2 * T])
        delta = sb("delta", [P, 2 * T])
        u = sb("u", [P, 2 * T])
        bc = sb("bc", [BCP, 2 * T], BF16)
        cw = sb("cw", [P, NB * NT * NE])

        stat = [sb(f"stat{k}", [P, NT, 6]) for k in range(4)]
        mv = [sb(f"mv{k}", [P, NT, 2]) for k in range(4)]
        vare = [sb(f"vare{k}", [P, NT]) for k in range(4)]
        rstd = [sb(f"rstd{k}", [P, NT]) for k in range(4)]
        xn1 = sb("xn1", [P, T])
        xnT = sb("xnT", [P, KC - 1 + T])
        resid = sb("resid", [BCP, T])
        midp = sb("midp", [BCP, T], BF16)
        reld = sb("reld", [P, T])
        expd = sb("expd", [P, T])
        onepd = sb("onepd", [P, T])
        lnd = sb("lnd", [P, T])
        dA = sb("dA", [P, P_DA, T])
        dBx = sb("dBx", [P, R_H, T])
        hs = sb("hs", [P, R_H, T])
        cs = sb("cs", [P, R_H, T])
        hC = sb("hC", [P, R_HC, T])
        quad = sb("quad", [P, 2, T])
        ysum = sb("ysum", [P, T])
        yg = sb("yg", [P, T])
        x1 = sb("x1", [P, T])
        xx = sb("xx", [P, T])
        xn2 = sb("xn2", [P, T])
        x2T = sb("x2T", [P, T])
        hid = sb("hid", [P, HF, T])
        x3T = [sb(f"x3T{k}", [P, T], FP32R) for k in range(2)]
        rmax = sb("rmax", [P, NT])
        rlog = sb("rlog", [P, NT, NE])
        rexp = sb("rexp", [P, NT, NE])
        rsum = sb("rsum", [P, NT])
        rinv = sb("rinv", [P, NT])
        prob = sb("prob", [P, NT, NE])
        pdif = sb("pdif", [P, NT, NE, NE])
        pbef = sb("pbef", [P, NT, NE * NE])
        rank = sb("rank", [P, NT, NE])
        topp = sb("topp", [P, NT, NE])
        tsum = sb("tsum", [P, NT])
        tsafe = sb("tsafe", [P, NT])
        tinv = sb("tinv", [P, NT])
        hm = sb("hm", [P, 2 * FE, T])
        ym = sb("ym", [P, 2, T])
        convb = ym[:, :, :].rearrange("p a (k e) -> p (a k) e", e=D)
        m1w = hid[:, :, :].rearrange("p k (e f) -> p (k e) f", f=FE * P)

        def bank(name):
            return ctx.enter_context(nc.psum_tensor(name, [P, T], FP32))
        pBC = [bank(f"pBC{k}") for k in range(3)]
        pG = [bank("pG0"), bank("pG1")]
        pH = [bank("pH0"), bank("pH1")]
        pO = bank("pO")

        w_loaded, x0_loaded, xr_loaded, wb_loaded = sem("w_loaded"), sem("x0_loaded"), sem("xr_loaded"), sem("wb_loaded")
        consts_set, expA_done, negA_done, convw_done = sem("consts_set"), sem("expA_done"), sem("negA_done"), sem("convw_done")
        deltaw_mm, deltaw_done = sem("deltaw_mm"), sem("deltaw_done")
        stats_done = [sem(f"stats_done{k}") for k in range(4)]
        mv_done = [sem(f"mv_done{k}") for k in range(4)]
        vare_done = [sem(f"vare_done{k}") for k in range(4)]
        rstd_done = [sem(f"rstd_done{k}") for k in range(4)]
        norm_done = [sem(f"norm_done{k}") for k in range(4)]
        t1_mm, xnT_done, conv_mm, xc_done = sem("t1_mm"), sem("xnT_done"), sem("conv_mm"), sem("xc_done")
        z_mm, zs_done, bc_mm, bchi_done = sem("z_mm"), sem("zs_done"), sem("bc_mm"), sem("bchi_done")
        resid_done, midp_done, bc_done = sem("resid_done"), sem("midp_done"), sem("bc_done")
        delta_mm, delta_read, expd_done, lnd_done = sem("delta_mm"), sem("delta_read"), sem("expd_done"), sem("lnd_done")
        onepd_done, limit_done, g_done, glim_done, log1p_done, delta_done, u_done = (
            sem("onepd_done"), sem("limit_done"), sem("g_done"), sem("glim_done"), sem("log1p_done"),
            sem("delta_done"), sem("u_done"))
        B_mm, C_mm, cs_done, dA_done, dBx_done = sem("B_mm"), sem("C_mm"), sem("cs_done"), sem("dA_done"), sem("dBx_done")
        scan_done, hC_done, quad_done, quarter_done, ysum_done = (
            sem("scan_done"), sem("hC_done"), sem("quad_done"), sem("quarter_done"), sem("ysum_done"))
        yg_done, out_mm, x1_done, xx_done = sem("yg_done"), sem("out_mm"), sem("x1_done"), sem("xx_done")
        t2_mm, x2T_done, hid_mm, hid_done, ffn_mm, res_done = (
            sem("t2_mm"), sem("x2T_done"), sem("hid_mm"), sem("hid_done"), sem("ffn_mm"), sem("res_done"))
        t3_mm, x3hi_done, x3T_done = sem("t3_mm"), sem("x3hi_done"), sem("x3T_done")
        m1w_split, rw_split = sem("m1w_split"), sem("rw_split")
        router_mm, rlog_done, rexp_done, rchain, cw_done = (
            sem("router_mm"), sem("rlog_done"), sem("rexp_done"), sem("rchain"), sem("cw_done"))
        ehid_mm, silu_done, eout_mm, ym_done, acc_done = (
            sem("ehid_mm"), sem("silu_done"), sem("eout_mm"), sem("ym_done"), sem("acc_done"))
        stored = sem("stored")
        parted = {e.engine: sem(f"parted{k}") for k, e in enumerate((nc.scalar, nc.vector, nc.gpsimd))}

        def of(t, b, n=T):
            places = t.shape[1] // n
            return t[:, bass.ds((b if places == NB else b % places) * n, n)]

        def tok(ap, j):
            return ap[:, j * D:(j + 1) * D]

        def apart(engine):
            engine.sem_inc(parted[engine.engine], 1)

        def B_bank(n):
            return pBC[2 * n % 3]

        def C_bank(n):
            return pBC[(2 * n + 1) % 3]

        def state_at(st, m):
            return (st[SCAN], m) if m < NS else (st[FRONT], m - NS)

        def place(n):
            return n if n < P_DA else n - 8

        FRONT_LOADS = 9
        BACK_LOADS = 7
        block = ctx.enter_context(nc.Block())

        xv = x.rearrange("b (j p) d -> p b j d", p=P)
        ov = out.rearrange("b (j p) d -> p b j d", p=P)
        xs4 = xs[:, :].rearrange("p (b j d) -> p b j d", b=NB, j=NT)

        @block.sync
        def _(sp):
            sp.dma_start(xs4[:, 0], xv[:, 0]).then_inc(x0_loaded, 16)
            sp.dma_start(vec[:, :], vecs).then_inc(w_loaded, 16)
            sp.dma_start(ident[:, :], identity).then_inc(w_loaded, 16)
            sp.dma_start(inw[:, :], in_wT).then_inc(w_loaded, 16)
            sp.dma_start(convb, conv_rows.unsqueeze(0).broadcast_to([P, KC, D])).then_inc(w_loaded, 16)
            sp.dma_start(xbcw[:, :], xbc_wT).then_inc(w_loaded, 16)
            sp.dma_start(xdtw[:, :], xdt_w).then_inc(w_loaded, 16)
            sp.dma_start(dtw[:, :], dt_wT).then_inc(w_loaded, 16)
            sp.dma_start(sel[:, :], select).then_inc(w_loaded, 16)
            sp.dma_start(tie[:, :], tie_limit).then_inc(w_loaded, 16)
            sp.dma_start(xs4[:, 1:NB], xv[:, 1:NB]).then_inc(xr_loaded, 16)
            sp.dma_start(outw[:, :], out_wT).then_inc(wb_loaded, 16)
            sp.dma_start(f1w[:, :], w1T).then_inc(wb_loaded, 16)
            sp.dma_start(f2w[:, :, :], w2T).then_inc(wb_loaded, 16)
            sp.dma_start(b2row[:, :], b2).then_inc(wb_loaded, 16)
            sp.dma_start(rw[:, :], router_w).then_inc(wb_loaded, 16)
            sp.dma_start(m1w, moe_w1).then_inc(wb_loaded, 16)
            sp.dma_start(m2w[:, :, :, :], moe_w2).then_inc(wb_loaded, 16)
            with sp.Fori(0, NB) as b:
                sp.wait_ge(acc_done, b * NE + NE)
                sp.dma_start(ov[:, bass.ds(b, 1)], xs4[:, bass.ds(b, 1)]).then_inc(stored, 16)
            sp.wait_ge(stored, 16 * NB)

        HIDDEN_AT = [2, 4, 6, 8, 10, 12, 14, 16]
        SILU_AT = [3, 5, 7, 9, 11, 13, 15, 17]
        OUT_AT = [5, 7, 9, 11, 13, 15, 17, 19]
        WEIGH_AT = [6, 8, 10, 12, 14, 16, 18, 20]

        CONV_AT = (1, 2, 3, 4, 4, 5, 6, 6)
        FFN_AT = (12, 12, 13, 13)
        BANK = dict(t1=0, conv=0, bc=0, delta=0, h1=0, h3=0, t3=1, router=1, out=1, z=1, t2=1, h0=1, h2=1, ffn=1)

        def experts_at(slots, n, st):
            for e, slot in enumerate(slots):
                if slot < NS and slot == n and st[EXPERT] is not None:
                    yield st[EXPERT], e
                if slot >= NS and slot - NS == n and st[TAIL] is not None:
                    yield st[TAIL], e

        @block.tensor
        def _(pe):
            turns = [("t1", (0,), FRONT, 0, xnT_done, 1, 1), ("t3", (1,), EXPERT, 1, x3T_done, 1, 1),
                     ("conv", CONV_AT, FRONT, 0, xc_done, 1, 1), ("router", (2,), EXPERT, 1, rlog_done, 1, 1),
                     ("out", (3,), MIDDLE, 1, x1_done, 1, 1), ("z", (6,), FRONT, 1, zs_done, 1, 1),
                     ("bc", (7,), FRONT, 0, resid_done, 1, 1), ("t2", (7,), MIDDLE, 1, x2T_done, 1, 1),
                     ("delta", (8,), FRONT, 0, delta_read, 1, 1),
                     ("h0", (8,), MIDDLE, 1, hid_done, HF, 1), ("h1", (9,), MIDDLE, 0, hid_done, HF, 2),
                     ("h2", (10,), MIDDLE, 1, hid_done, HF, 3), ("h3", (11,), MIDDLE, 0, hid_done, HF, 4),
                     ("ffn", FFN_AT, MIDDLE, 1, res_done, 1, 1)]
            assert [(t[0], t[3]) for t in turns if t[3] != BANK[t[0]]] == []

            def wait_bank(i, k):
                for back in range(1, 2 * len(turns)):
                    j = k - back
                    r = i if j >= 0 else i - 1
                    if isinstance(r, int) and r < FIRST_ROUND:
                        return
                    _, _, stage, at, read, per, nth = turns[j % len(turns)]
                    b = stages(r)[stage]
                    if at == turns[k][3] and b is not None:
                        pe.wait_ge(read, b * per + nth)
                        return

            def transpose4(dst, src, done):
                for j in range(NT):
                    last = nc.tensor.transpose(tok(dst, j), tok(src, j), ident[:, :])
                last.then_inc(done, 1)

            pe.wait_ge(w_loaded, 16 * FRONT_LOADS)
            nc.tensor.matmul(pG[0][:, 0:D], xdtw[:, :], dtw[:, :], start=True, stop=True).then_inc(deltaw_mm, 1)
            pe.wait_ge(deltaw_done, 1)

            def product(name, b, part):
                pg = pG[BANK[name]]
                if name == "router":
                    pe.wait_ge(x3T_done, b + 1)
                    if isinstance(b, int) and b == 0:
                        pe.wait_ge(rw_split, 2)
                    for j in range(NT):
                        for k, (a, w) in enumerate(((0, 0), (0, 1), (1, 0))):
                            last = nc.tensor.matmul(pg[:, j * NE:(j + 1) * NE], x3T[a][:, j * P:(j + 1) * P],
                                                    rwp[w][:, :], start=(k == 0), stop=(k == 2))
                    last.then_inc(router_mm, 1)
                elif name == "out":
                    pe.wait_ge(yg_done, b + 1)
                    for j in range(NT):
                        last = nc.tensor.matmul(tok(pg, j), yg[:, j * P:(j + 1) * P], outw[:, :], start=True, stop=True)
                    last.then_inc(out_mm, 1)
                elif name == "t1":
                    pe.wait_ge(norm_done[1], b + 1)
                    transpose4(pg, xn1, t1_mm)
                elif name == "t2":
                    pe.wait_ge(norm_done[2], b + 1)
                    transpose4(pg, xn2, t2_mm)
                elif name == "t3":
                    pe.wait_ge(norm_done[3], b + 1)
                    transpose4(pg, xn2, t3_mm)
                elif name == "conv":
                    if part == 0:
                        pe.wait_ge(xnT_done, b + 1)
                        if isinstance(b, int) and b == 0:
                            pe.wait_ge(convw_done, 1)
                    last = nc.tensor.matmul(pg[:, :], convw[:, part, :], xnT[:, part:part + T],
                                            start=(part == 0), stop=(part == KC - 1))
                    if part == KC - 1:
                        last.then_inc(conv_mm, 1)
                elif name == "z":
                    nc.tensor.matmul(pg[:, :], inw[:, D:2 * D], xnT[:, KC - 1:], start=True, stop=True).then_inc(z_mm, 1)
                elif name == "bc":
                    pe.wait_ge(xc_done, b + 1)
                    nc.tensor.matmul(pg[0:BCP, :], xbcw[:, :], of(xc, b), start=True, stop=True).then_inc(bc_mm, 1)
                elif name == "delta":
                    nc.tensor.matmul(pg[:, :], deltaw[:, :], of(xc, b), start=True, stop=True).then_inc(delta_mm, 1)
                elif name == "ffn":
                    if part == 0:
                        pe.wait_ge(hid_done, HF * b + HF)
                    for k in range(HF):
                        nc.tensor.matmul(tok(pg, part), hid[:, k, part * P:(part + 1) * P], f2w[:, k, :],
                                         start=(k == 0), stop=False)
                    last = nc.tensor.matmul(tok(pg, part), ones[:, :], b2row[:, :], start=False, stop=True)
                    if part == NT - 1:
                        last.then_inc(ffn_mm, 1)
                else:
                    k = int(name[1])
                    if k == 0:
                        pe.wait_ge(x2T_done, b + 1)
                    nc.tensor.matmul(pg[:, :], f1w[:, k * P:(k + 1) * P], x2T[:, :], start=True, stop=True).then_inc(hid_mm, 1)

            def broadcast(row, bank, b, done):
                nc.tensor.matmul(bank[:, :], sel[:, row:row + 1].broadcast_to([BCP, P]), of(bc, b), start=True, stop=True).then_inc(done, 1)

            def broadcast_B(b, n):
                if n == 0:
                    pe.wait_ge(bc_done, 2 * b + 2)
                    if not isinstance(b, int) or b >= 1:
                        pe.wait_ge(dBx_done, b * NS)
                elif not isinstance(b, int) or NS * b + n >= 2:
                    pe.wait_ge(cs_done, b * NS + n - 1)
                broadcast(n, B_bank(n), b, B_mm)

            def broadcast_C(b, n):
                if n == 0:
                    if not isinstance(b, int) or b >= 1:
                        pe.wait_ge(cs_done, b * NS)
                else:
                    pe.wait_ge(dBx_done, b * NS + n)
                broadcast(NS + n, C_bank(n), b, C_mm)

            def expert_hidden(b, e):
                if e == 0:
                    pe.wait_ge(x3T_done, b + 1)
                    if isinstance(b, int) and b == 0:
                        pe.wait_ge(m1w_split, 2)
                for f in range(FE):
                    if not isinstance(b, int) or b * NE + e >= 1:
                        pe.wait_ge(silu_done, b * NE * FE + e * FE + f - 1)
                    for k, (w, a) in enumerate(((0, 0), (1, 0), (0, 1))):
                        last = nc.tensor.matmul(pH[f][:, :], m1wp[w][:, e, f * P:(f + 1) * P], x3T[a][:, :],
                                                start=(k == 0), stop=(k == 2))
                    last.then_inc(ehid_mm, 1)

            def expert_out(b, e):
                pe.wait_ge(silu_done, b * NE * FE + e * FE + 2)
                if not isinstance(b, int) or b * NE + e >= 1:
                    pe.wait_ge(ym_done, b * NE + e)
                for j in range(NT):
                    for f in range(FE):
                        last = nc.tensor.matmul(tok(pO, j), hm[:, (e % 2) * FE + f, j * P:(j + 1) * P], m2w[:, e, f, :],
                                                start=(f == 0), stop=(f == FE - 1))
                last.then_inc(eout_mm, 1)

            def body(i):
                st = stages(i)
                if isinstance(i, int) and i == 1:
                    pe.wait_ge(wb_loaded, 16 * BACK_LOADS)
                for n in range(NS):
                    b, m = state_at(st, n + 1)
                    if b is not None:
                        broadcast_C(b, m)
                    b, m = state_at(st, n + 2)
                    if b is not None:
                        broadcast_B(b, m)
                    for k, (name, slots, stage, *_) in enumerate(turns):
                        for part, slot in enumerate(slots):
                            if slot == n and st[stage] is not None:
                                if part == 0:
                                    wait_bank(i, k)
                                product(name, st[stage], part)
                    for b, e in experts_at(HIDDEN_AT, n, st):
                        expert_hidden(b, e)
                    for b, e in experts_at(OUT_AT, n, st):
                        expert_out(b, e)

            rounds(pe, body)

        @block.scalar
        def _(act):
            act.wait_ge(w_loaded, 16 * FRONT_LOADS)
            nc.scalar.activation(expA[:, :], vec[:, V_ALOG:V_ALOG + NS], ACT.Exp).then_inc(expA_done, 1)
            act.wait_ge(deltaw_mm, 1)
            nc.scalar.activation(deltaw[:, :], pG[0][:, 0:D], ACT.Copy).then_inc(deltaw_done, 1)

            DECAYS_BEFORE = {0: (3, 4, 5), 1: (6, 7), 4: (10, 11), 10: (13, 14), 11: (15,)}
            DECAYS_AFTER = {3: (8, 9), 9: (12,), 15: (16, 17, 18)}

            def decay(b, n):
                if n == 0:
                    act.wait_ge(delta_done, b + 1)
                    if isinstance(b, int) and b == 0:
                        act.wait_ge(negA_done, 1)
                before = n - 8 if n >= P_DA else n + 8 - NS if 4 <= n < 8 else n - NS
                if not isinstance(b, int) or NS * b + before >= 0:
                    act.wait_ge(scan_done, b * NS + before + 1)
                apart(act)
                nc.scalar.activation(dA[:, place(n), :], of(delta, b), ACT.Exp,
                                     scale=negA[:, n:n + 1]).then_inc(dA_done, 1)

            def body(i):
                st = stages(i)
                front, middle, expert = st[FRONT], st[MIDDLE], st[EXPERT]
                for n in range(NS):
                    b, m = state_at(st, n + 1)
                    if b is not None:
                        act.wait_ge(C_mm, b * NS + m + 1)
                        if not isinstance(b, int) or NS * b + m >= R_H:
                            act.wait_ge(hC_done, b * NS + m - R_H + 1)
                        nc.scalar.activation(cs[:, m % R_H, :], C_bank(m)[:, :], ACT.Copy).then_inc(cs_done, 1)
                    for m in DECAYS_BEFORE.get(n, ()):
                        b, m = state_at(st, m)
                        if b is not None:
                            decay(b, m)
                    if front is not None and n == 0:
                        act.wait_ge(t1_mm, front + 1)
                        if isinstance(front, int) and front == 0:
                            act.wait_ge(consts_set, 1)
                        else:
                            act.wait_ge(z_mm, front)
                        nc.scalar.activation(xnT[:, KC - 1:], pG[BANK["t1"]][:, :], ACT.Identity,
                                             scale=vec[:, V_G1:V_G1 + 1], bias=vec[:, V_B1:V_B1 + 1]).then_inc(xnT_done, 1)
                    if expert is not None and n == 1:
                        act.wait_ge(t3_mm, expert + 1)
                        if not isinstance(expert, int) or expert >= 1:
                            act.wait_ge(ehid_mm, expert * NE * FE)
                        nc.scalar.activation(x3T[0][:, :], pG[BANK["t3"]][:, :], ACT.Copy).then_inc(x3hi_done, 1)
                    if expert is not None and n == 4:
                        act.wait_ge(rlog_done, expert + 1)
                        nc.scalar.activation(rexp[:, :, :], rlog[:, :, :], ACT.Exp).then_inc(rexp_done, 1)
                    if front is not None and n == 11:
                        act.wait_ge(expd_done, front + 1)
                        apart(act)
                        nc.scalar.activation(of(u, front), expd[:, :], ACT.Square, scale=HALF_ROOT).then_inc(limit_done, 1)
                        act.wait_ge(onepd_done, front + 1)
                        nc.scalar.activation(lnd[:, :], onepd[:, :], ACT.Ln).then_inc(lnd_done, 1)
                    if front is not None and n == 6:
                        act.wait_ge(conv_mm, front + 1)
                        if not isinstance(front, int) or front >= 2:
                            act.wait_ge(ysum_done, 4 * front - 7)
                            act.wait_ge(u_done, front - 1)
                            act.wait_ge(delta_mm, front - 1)
                        apart(act)
                        nc.scalar.activation(of(xc, front), pG[BANK["conv"]][:, :], ACT.Silu,
                                             bias=vec[:, V_CONVB:V_CONVB + 1]).then_inc(xc_done, 1)
                        act.wait_ge(z_mm, front + 1)
                        if not isinstance(front, int) or front >= 2:
                            act.wait_ge(yg_done, front - 1)
                        apart(act)
                        nc.scalar.activation(of(zs, front), pG[BANK["z"]][:, :], ACT.Silu).then_inc(zs_done, 1)
                    if front is not None and n == 7:
                        act.wait_ge(bc_mm, front + 1)
                        apart(act)
                        nc.scalar.activation(of(bc, front), pG[BANK["bc"]][0:BCP, :], ACT.Copy).then_inc(bchi_done, 1)
                    if middle is not None and n == 7:
                        act.wait_ge(t2_mm, middle + 1)
                        nc.scalar.activation(x2T[:, :], pG[BANK["t2"]][:, :], ACT.Identity, scale=vec[:, V_G2:V_G2 + 1],
                                             bias=vec[:, V_B2:V_B2 + 1]).then_inc(x2T_done, 1)
                    if front is not None and n == 8:
                        bias = vec[:, V_DTB:V_DTB + 1]
                        act.wait_ge(delta_mm, front + 1)
                        nc.scalar.activation(expd[:, :], pG[BANK["delta"]][:, :], ACT.Abs, bias=bias)
                        nc.scalar.activation(reld[:, :], pG[BANK["delta"]][:, :], ACT.Relu, bias=bias).then_inc(delta_read, 1)
                    if middle is not None and 8 <= n < 8 + HF:
                        k = n - 8
                        act.wait_ge(hid_mm, middle * HF + k + 1)
                        if isinstance(middle, int) and middle == 0:
                            act.wait_ge(m1w_split, 2)
                        nc.scalar.activation(hid[:, k, :], pG[BANK[f"h{k}"]][:, :], ACT.Relu,
                                             bias=vec[:, V_FB + k:V_FB + k + 1]).then_inc(hid_done, 1)
                    for b, e in experts_at(SILU_AT, n, st):
                        for f in range(FE):
                            act.wait_ge(ehid_mm, b * NE * FE + e * FE + f + 1)
                            if not isinstance(b, int) or b * NE + e >= 2:
                                act.wait_ge(eout_mm, b * NE + e - 1)
                            nc.scalar.activation(hm[:, (e % 2) * FE + f, :], pH[f][:, :], ACT.Silu).then_inc(silu_done, 1)
                    if front is not None and n == 9:
                        act.wait_ge(delta_read, front + 1)
                        nc.scalar.activation(expd[:, :], expd[:, :], ACT.Exp, scale=-1.0).then_inc(expd_done, 1)
                    if front is not None and n == 10:
                        act.wait_ge(resid_done, front + 1)
                        nc.scalar.activation(midp[64:96, :], resid[64:96, :], ACT.Copy).then_inc(midp_done, 1)
                        apart(act)
                        nc.scalar.activation(bc[32:64, bass.ds(front % 2 * T, T)], resid[32:64, :], ACT.Copy).then_inc(bc_done, 1)
                    for m in DECAYS_AFTER.get(n, ()):
                        b, m = state_at(st, m)
                        if b is not None:
                            decay(b, m)

            rounds(act, body)

        @block.vector
        def _(dve):
            nc.vector.memset(xnT[:, 0:KC - 1], 0.0)
            nc.vector.memset(ones[:, :], 1.0)
            nc.vector.memset(neghalf[:, :], -0.5).then_inc(consts_set, 1)
            dve.wait_ge(expA_done, 1)
            dve.wait_ge(convw_done, 1)
            nc.vector.tensor_scalar(negA[:, :], expA[:, :], -1.0, None, ALU.mult).then_inc(negA_done, 1)

            def split(parts, whole, done):
                nc.vector.tensor_copy(parts[0], whole).then_inc(done, 1)
                dve.wait_ge(done, 1)
                nc.vector.tensor_tensor(parts[1], whole, parts[0].bitcast(FP32), ALU.subtract).then_inc(done, 1)

            def statistics(k, b, src):
                apart(dve)
                for j in range(NT):
                    last = nc.vector.bn_stats(stat[k][:, j, :], tok(src, j))
                last.then_inc(stats_done[k], 1)
                dve.wait_ge(stats_done[k], b + 1)
                apart(dve)
                for j in range(NT):
                    last = nc.vector.bn_aggr(mv[k][:, j, :], stat[k][:, j, :])
                last.then_inc(mv_done[k], 1)

            def normalise(k, b, dst, src):
                dve.wait_ge(rstd_done[k], b + 1)
                apart(dve)
                for j in range(NT):
                    last = nc.vector.tensor_scalar(tok(dst, j), tok(src, j), mv[k][:, j, 0:1], rstd[k][:, j:j + 1],
                                                   ALU.subtract, ALU.mult)
                last.then_inc(norm_done[k], 1)

            def drive(b, n):
                if n == 0:
                    dve.wait_ge(u_done, b + 1)
                dve.wait_ge(B_mm, b * NS + n + 1)
                if not isinstance(b, int) or NS * b + n >= R_H:
                    dve.wait_ge(scan_done, b * NS + n - R_H + 1)
                nc.vector.tensor_tensor(dBx[:, n % R_H, :], of(u, b), B_bank(n)[:, :], ALU.mult).then_inc(dBx_done, 1)

            def sum_states(b, q):
                a = 4 * q % R_HC
                dve.wait_ge(hC_done, b * NS + 4 * q + 4)
                if not isinstance(b, int) or 4 * b + q >= 1:
                    dve.wait_ge(ysum_done, 4 * b + q)
                nc.vector.tensor_tensor(quad[:, :, :], hC[:, a:a + 2, :], hC[:, a + 2:a + 4, :], ALU.add).then_inc(quad_done, 1)
                dve.wait_ge(quad_done, 4 * b + q + 1)
                nc.vector.tensor_tensor(quad[:, 0, :], quad[:, 0, :], quad[:, 1, :], ALU.add).then_inc(quarter_done, 1)
                dve.wait_ge(quarter_done, 4 * b + q + 1)
                if q == 0:
                    if not isinstance(b, int) or b >= 1:
                        dve.wait_ge(yg_done, b)
                    nc.vector.scalar_tensor_tensor(out=ysum[:, :], in0=of(xc, b), scalar=vec[:, V_D:V_D + 1],
                                                   in1=quad[:, 0, :], op0=ALU.mult, op1=ALU.add).then_inc(ysum_done, 1)
                else:
                    nc.vector.tensor_tensor(ysum[:, :], ysum[:, :], quad[:, 0, :],
                                            ALU.add).then_inc(ysum_done, 1)

            def router_head(b):
                dve.wait_ge(router_mm, b + 1)
                logits = pG[BANK["router"]][:, 0:NT * NE].rearrange("p (j e) -> p j e", j=NT)
                nc.vector.tensor_reduce(rmax[:, :], logits, AX.X, ALU.max).then_inc(rchain, 1)
                dve.wait_ge(rchain, R_CHAIN * b + 1)
                nc.vector.tensor_tensor(rlog[:, :, :], logits, rmax[:, :].unsqueeze(2).broadcast_to([P, NT, NE]),
                                        ALU.subtract).then_inc(rlog_done, 1)

            def router_tail(b):
                count = [1]

                def link(op):
                    count[0] += 1
                    op.then_inc(rchain, 1)
                    dve.wait_ge(rchain, R_CHAIN * b + count[0])

                def over_experts(t):
                    return t[:, :].unsqueeze(2).broadcast_to([P, NT, NE])

                dve.wait_ge(rexp_done, b + 1)
                link(nc.vector.tensor_reduce(rsum[:, :], rexp[:, :, :], AX.X, ALU.add))
                link(nc.vector.reciprocal(rinv[:, :], rsum[:, :]))
                link(nc.vector.tensor_tensor(prob[:, :, :], rexp[:, :, :], over_experts(rinv), ALU.mult))
                link(nc.vector.tensor_tensor(pdif[:, :, :, :], prob[:, :, :].unsqueeze(2).broadcast_to([P, NT, NE, NE]),
                                             prob[:, :, :].unsqueeze(3).broadcast_to([P, NT, NE, NE]), ALU.subtract))
                link(nc.vector.tensor_tensor(pbef[:, :, :], pdif[:, :, :, :].rearrange("p t e j -> p t (e j)"),
                                             tie[:, :].unsqueeze(1).broadcast_to([P, NT, NE * NE]), ALU.is_ge))
                link(nc.vector.tensor_reduce(rank[:, :, :], pbef[:, :, :].rearrange("p t (e j) -> p t e j", e=NE),
                                             AX.X, ALU.add))
                link(nc.vector.scalar_tensor_tensor(out=topp[:, :, :], in0=rank[:, :, :], scalar=2.0, in1=prob[:, :, :],
                                                    op0=ALU.is_lt, op1=ALU.mult))
                link(nc.vector.tensor_reduce(tsum[:, :], topp[:, :, :], AX.X, ALU.add))
                link(nc.vector.tensor_scalar(tsafe[:, :], tsum[:, :], EPS_TOP, None, ALU.max))
                link(nc.vector.reciprocal(tinv[:, :], tsafe[:, :]))
                assert count[0] == R_CHAIN
                nc.vector.tensor_tensor(of(cw, b, NT * NE).rearrange("p (j e) -> p j e", j=NT), topp[:, :, :],
                                        over_experts(tinv), ALU.mult).then_inc(cw_done, 1)

            def weigh(b, e):
                dve.wait_ge(eout_mm, b * NE + e + 1)
                if e == 0:
                    dve.wait_ge(cw_done, b + 1)
                if not isinstance(b, int) or b * NE + e >= 2:
                    dve.wait_ge(acc_done, b * NE + e - 1)
                w = of(cw, b, NT * NE).rearrange("p (j e) -> p j e", j=NT)[:, :, e:e + 1].broadcast_to([P, NT, D])
                nc.vector.tensor_tensor(ym[:, e % 2, :].rearrange("p (j d) -> p j d", j=NT),
                                        pO[:, :].rearrange("p (j d) -> p j d", j=NT), w, ALU.mult).then_inc(ym_done, 1)

            def body(i):
                st = stages(i)
                norms, front, scan, middle, expert = st[:TAIL]
                for n in range(NS):
                    b, m = state_at(st, n + 1)
                    if b is not None:
                        drive(b, m)
                    if scan is not None:
                        dve.wait_ge(dBx_done, scan * NS + n + 1)
                        dve.wait_ge(dA_done, scan * NS + n + 1)
                        if not isinstance(scan, int) or NS * scan + n >= R_H:
                            dve.wait_ge(hC_done, scan * NS + n - R_H + 1)
                        nc.vector.tensor_tensor_scan(hs[:, n % R_H, :], dA[:, place(n), :], dBx[:, n % R_H, :], 0.0,
                                                     ALU.mult, ALU.add).then_inc(scan_done, 1)
                        if n in (6, 10, 14):
                            sum_states(scan, n // 4 - 1)
                    if n == 0 and middle is not None:
                        sum_states(middle, 3)
                    if n == 1 and expert is not None:
                        dve.wait_ge(x3hi_done, expert + 1)
                        nc.vector.tensor_tensor(x3T[1][:, :], pG[BANK["t3"]][:, :], x3T[0][:, :].bitcast(FP32),
                                                ALU.subtract).then_inc(x3T_done, 1)
                    if n == 3:
                        if expert is not None:
                            router_head(expert)
                        if middle is not None:
                            dve.wait_ge(out_mm, middle + 1)
                            if not isinstance(middle, int) or middle >= 1:
                                dve.wait_ge(xx_done, middle)
                            nc.vector.tensor_tensor(x1[:, :], of(xa, middle), pG[BANK["out"]][:, :], ALU.add).then_inc(x1_done, 1)
                            dve.wait_ge(x1_done, middle + 1)
                            statistics(2, middle, x1)
                    if n == 5:
                        if middle is not None:
                            if not isinstance(middle, int) or middle >= 1:
                                dve.wait_ge(t3_mm, middle)
                            normalise(2, middle, xn2, x1)
                        if expert is not None:
                            router_tail(expert)
                    if n == 7 and front is not None:
                        dve.wait_ge(bchi_done, front + 1)
                        nc.vector.tensor_tensor(resid[:, :], pG[BANK["bc"]][0:BCP, :], of(bc, front),
                                                ALU.subtract).then_inc(resid_done, 1)
                    if n == 10 and front is not None:
                        dve.wait_ge(expd_done, front + 1)
                        nc.vector.tensor_scalar(onepd[:, :], expd[:, :], 1.0, None, ALU.add).then_inc(onepd_done, 1)
                    if n == 11 and front is not None:
                        dve.wait_ge(midp_done, front + 1)
                        nc.vector.tensor_tensor(bc[64:96, bass.ds(front % 2 * T, T)], resid[64:96, :], midp[64:96, :],
                                                ALU.subtract).then_inc(bc_done, 1)
                    if n == 12 and front is not None:
                        dve.wait_ge(lnd_done, front + 1)
                        nc.vector.scalar_tensor_tensor(out=lnd[:, :], in0=onepd[:, :], scalar=-1.0, in1=lnd[:, :],
                                                       op0=ALU.add, op1=ALU.subtract).then_inc(g_done, 1)
                        dve.wait_ge(g_done, front + 1)
                        dve.wait_ge(limit_done, front + 1)
                        nc.vector.scalar_tensor_tensor(out=lnd[:, :], in0=lnd[:, :], scalar=0.0, in1=of(u, front),
                                                       op0=ALU.max, op1=ALU.min).then_inc(glim_done, 1)
                    if n == 9 and norms is not None:
                        if isinstance(i, int) and i == FIRST_ROUND:
                            dve.wait_ge(x0_loaded, 16)
                        if isinstance(i, int) and i == FIRST_ROUND + 1:
                            dve.wait_ge(xr_loaded, 16)
                        statistics(0, norms, of(xs, norms))
                    if n == 11 and norms is not None:
                        normalise(0, norms, of(xa, norms), of(xs, norms))
                        dve.wait_ge(norm_done[0], norms + 1)
                        statistics(1, norms, of(xa, norms))
                    if n == 13 and norms is not None:
                        if not isinstance(norms, int) or norms >= 1:
                            dve.wait_ge(t1_mm, norms)
                        normalise(1, norms, xn1, of(xa, norms))
                    if n == 13 and middle is not None:
                        dve.wait_ge(ffn_mm, middle + 1)
                        dve.wait_ge(xx_done, middle + 1)
                        nc.vector.tensor_tensor(of(xs, middle), xx[:, :], pG[BANK["ffn"]][:, :], ALU.add).then_inc(res_done, 1)
                        dve.wait_ge(res_done, middle + 1)
                        statistics(3, middle, of(xs, middle))
                    if n == 15 and middle is not None:
                        dve.wait_ge(t2_mm, middle + 1)
                        normalise(3, middle, xn2, of(xs, middle))
                    for b, e in experts_at(WEIGH_AT, n, st):
                        weigh(b, e)
                if isinstance(i, int) and i == 0:
                    dve.wait_ge(wb_loaded, 16 * BACK_LOADS)
                    split([w[:, :] for w in rwp], rw[:, :], rw_split)
                    split([w[:, :, :] for w in m1wp], m1w, m1w_split)

            rounds(dve, body)

        @block.gpsimd
        def _(pool):
            pool.wait_ge(w_loaded, 16 * FRONT_LOADS)
            nc.gpsimd.tensor_tensor(convw[:, :, :], inw[:, 0:D].unsqueeze(1).broadcast_to([P, KC, D]), convb,
                                    ALU.mult).then_inc(convw_done, 1)
            pool.wait_ge(consts_set, 1)

            def inverse_deviation(k, b):
                pool.wait_ge(mv_done[k], b + 1)
                apart(pool)
                nc.gpsimd.tensor_scalar(vare[k][:, :], mv[k][:, :, 1], EPS_LN, 1.0, ALU.add, ALU.mult).then_inc(vare_done[k], 1)
                pool.wait_ge(vare_done[k], b + 1)
                nc.gpsimd.tensor_tensor(rstd[k][:, :], vare[k][:, :], neghalf[:, :], ALU.pow).then_inc(rstd_done[k], 1)

            def add_expert(b, e):
                pool.wait_ge(ym_done, b * NE + e + 1)
                if not isinstance(b, int) or b * NE + e >= 1:
                    pool.wait_ge(acc_done, b * NE + e)
                apart(pool)
                nc.gpsimd.tensor_tensor(of(xs, b), of(xs, b), ym[:, e % 2, :], ALU.add).then_inc(acc_done, 1)

            def body(i):
                st = stages(i)
                norms, front, scan, middle = st[NORMS], st[FRONT], st[SCAN], st[MIDDLE]
                for n in range(NS):
                    if scan is not None:
                        pool.wait_ge(scan_done, scan * NS + n + 1)
                        pool.wait_ge(cs_done, scan * NS + n + 1)
                        if not isinstance(scan, int) or NS * scan + n >= R_HC:
                            pool.wait_ge(quad_done, 4 * scan + n // 4 - 1)
                        nc.gpsimd.tensor_tensor(hC[:, n % R_HC, :], hs[:, n % R_H, :], cs[:, n % R_H, :],
                                                ALU.mult).then_inc(hC_done, 1)
                    if n == 1 and middle is not None:
                        pool.wait_ge(ysum_done, 4 * middle + 4)
                        if not isinstance(middle, int) or middle >= 1:
                            pool.wait_ge(out_mm, middle)
                        apart(pool)
                        nc.gpsimd.tensor_tensor(yg[:, :], ysum[:, :], of(zs, middle), ALU.mult).then_inc(yg_done, 1)
                    if n == 4 and middle is not None:
                        inverse_deviation(2, middle)
                        apart(pool)
                        nc.gpsimd.tensor_tensor(xx[:, :], of(xs, middle), x1[:, :], ALU.add).then_inc(xx_done, 1)
                    if n == 12 and front is not None:
                        pool.wait_ge(glim_done, front + 1)
                        nc.gpsimd.tensor_tensor(lnd[:, :], expd[:, :], lnd[:, :], ALU.subtract).then_inc(log1p_done, 1)
                        pool.wait_ge(log1p_done, front + 1)
                        apart(pool)
                        nc.gpsimd.tensor_tensor(of(delta, front), lnd[:, :], reld[:, :], ALU.add).then_inc(delta_done, 1)
                        pool.wait_ge(delta_done, front + 1)
                        apart(pool)
                        nc.gpsimd.tensor_tensor(of(u, front), of(delta, front), of(xc, front), ALU.mult).then_inc(u_done, 1)
                    if n == 10 and norms is not None:
                        inverse_deviation(0, norms)
                    if n == 12 and norms is not None:
                        inverse_deviation(1, norms)
                    if n == 14 and middle is not None:
                        inverse_deviation(3, middle)
                    for b, e in experts_at(WEIGH_AT, n, st):
                        add_expert(b, e)

            rounds(pool, body)


R_CHAIN = 11


def kernel(**inputs):
    import numpy as np
    import ml_dtypes
    import concourse.bacc as bacc
    from concourse.bass_utils import run_bass_kernel_spmd

    a = {k: np.asarray(v) for k, v in inputs.items()}
    g = lambda name: a["L0_attn_" + name]
    columns = [g("conv_b"), g("dt_proj_b"), g("D_param"), g("ln1_g"), g("ln1_b"), g("ln2_g"), g("ln2_b")]
    columns += list(g("b1").reshape(HF, P))
    xp = g("x_proj_w")
    arrays = dict(
        x=g("x"),
        vecs=np.concatenate([np.stack(columns, axis=1), g("A_log")], axis=1),
        in_wT=g("in_proj_w").T,
        conv_rows=g("conv_w").T,
        xbc_wT=np.concatenate([xp[8:40]] * 3, axis=0).T,
        xdt_w=xp[0:8],
        dt_wT=g("dt_proj_w").T,
        out_wT=g("out_proj_w").T,
        w1T=g("w1").T,
        w2T=g("w2").T.reshape(HF, P, D).transpose(1, 0, 2),
        b2=g("b2").reshape(1, D),
        router_w=a["L0_ffn_router_w"],
        moe_w1=a["L0_ffn_w1"].transpose(1, 0, 2),
        moe_w2=a["L0_ffn_w2"].reshape(NE, FE, P, D).transpose(2, 0, 1, 3),
        identity=np.eye(P, dtype=np.float32),
        select=(np.arange(BCP)[:, None] % 32 == np.arange(32)[None, :]).astype(ml_dtypes.bfloat16),
        tie_limit=np.broadcast_to(np.where(np.arange(NE)[None, :] < np.arange(NE)[:, None], np.float32(0),
                                           np.finfo(np.float32).tiny).reshape(1, NE * NE), (P, NE * NE)),
    )
    arrays = {k: np.ascontiguousarray(v) for k, v in arrays.items()}
    nc = bacc.Bacc("TRN2", target_bir_lowering=False, num_devices=1)
    args = [nc.dram_tensor(f"in_{k}", v.shape, mybir.dt.from_np(v.dtype), kind="ExternalInput").ap()
            for k, v in arrays.items()]
    out = nc.dram_tensor("out_0", (NB, T, D), FP32, kind="ExternalOutput").ap()
    mamba_moe(nc, *args, out)
    r = run_bass_kernel_spmd(nc, [{f"in_{k}": v for k, v in arrays.items()}], core_ids=[0])
    return r.results[0]["out_0"]
```

```python
import concourse.bass as bass
from concourse import mybir
from contextlib import ExitStack

FP32 = mybir.dt.float32
FP32R = mybir.dt.float32r
BF16 = mybir.dt.bfloat16
ALU = mybir.AluOpType
ACT = mybir.ActivationFunctionType
AX = mybir.AxisListType

NB, T, D = 8, 512, 128
P = 128
NT = T // P
NS = 16
KC = 8
HF = 4
NE, FE = 8, 2
EPS_LN, EPS_TOP = 1e-5, 1e-9
BCP = 96

V_CONVB, V_DTB, V_D, V_G1, V_B1, V_G2, V_B2, V_FB, V_ALOG = 0, 1, 2, 3, 4, 5, 6, 7, 11
NV = V_ALOG + NS

R_DBX, R_H, R_HC = 2, 4, 8

FIRST_ROUND, FULL_FROM, FULL_TO, ROUNDS = -2, 4, NB - 2, NB + 3


NORMS, FRONT, SCAN, MIDDLE, EXPERT, TAIL = range(6)


def stages(i):
    out = []
    for b in (i + 2, i + 1, i, i - 1, i - 2, i - 3):
        if isinstance(b, int) and not 0 <= b < NB:
            b = None
        out.append(b)
    return out


def rounds(engine, body):
    for i in range(FIRST_ROUND, FULL_FROM):
        body(i)
    with engine.Fori(FULL_FROM, FULL_TO) as i:
        body(i)
    for i in range(FULL_TO, ROUNDS):
        body(i)


def mamba_moe(nc, x, vecs, in_wT, conv_rows, xbc_wT, xdt_w, dt_wT, out_wT, w1T, w2T, b2, router_w,
              moe_w1, moe_w2, identity, select, tie_limit, out):
    ctx = ExitStack()
    with ctx:
        def sb(name, shape, dt=FP32):
            return ctx.enter_context(nc.sbuf_tensor(name, shape, dt))

        def sem(name):
            return ctx.enter_context(nc.semaphore(name))

        vec = sb("vec", [P, NV])
        inw = sb("inw", [P, 2 * D])
        convw = [sb(f"convw{k}", [P, KC, D], FP32R) for k in range(2)]
        zw = [sb(f"zw{k}", [P, D], FP32R) for k in range(2)]
        xbcw = sb("xbcw", [P, BCP])
        xdtw = sb("xdtw", [8, D])
        dtw = sb("dtw", [8, D])
        deltaw = sb("deltaw", [P, D])
        outw = sb("outw", [P, D])
        f1w = sb("f1w", [P, HF * P])
        f2w = sb("f2w", [P, HF, D])
        b2all = sb("b2all", [P, D])
        rw = sb("rw", [P, NE])
        rwp = [sb(f"rwp{k}", [P, NE], FP32R) for k in range(2)]
        m1wp = [sb(f"m1wp{k}", [P, NE, FE * P], FP32R) for k in range(2)]
        m2w = sb("m2w", [P, NE, FE, D])
        ident = sb("ident", [P, P])
        sel = sb("sel", [BCP, 2 * NS], BF16)
        tie = sb("tie", [P, NE * NE])
        expA = sb("expA", [P, NS])
        negA = sb("negA", [P, NS])
        neghalf = sb("neghalf", [P, NT])

        xs = sb("xs", [P, NB * T])
        xa = sb("xa", [P, 4 * T])
        xc = sb("xc", [P, 2 * T])
        zs = sb("zs", [P, 2 * T])
        delta = sb("delta", [P, 2 * T])
        u = sb("u", [P, 2 * T])
        bc = sb("bc", [BCP, 2 * T], BF16)
        cw = sb("cw", [P, NB * NT * NE])

        stat = [sb(f"stat{k}", [P, NT, 6]) for k in range(4)]
        mv = [sb(f"mv{k}", [P, NT, 2]) for k in range(4)]
        vare = [sb(f"vare{k}", [P, NT]) for k in range(4)]
        rstd = [sb(f"rstd{k}", [P, NT]) for k in range(4)]
        xn1 = sb("xn1", [P, T])
        xnT = [sb(f"xnT{k}", [P, KC - 1 + T], FP32R) for k in range(2)]
        resid = sb("resid", [BCP, T])
        midp = sb("midp", [BCP, T], BF16)
        reld = sb("reld", [P, T])
        expd = sb("expd", [P, T])
        lnd = sb("lnd", [P, T])
        dA = sb("dA", [P, NS, T])
        dBx = sb("dBx", [P, R_DBX, T])
        hs = sb("hs", [P, R_H, T])
        cs = sb("cs", [P, R_H, T])
        hC = sb("hC", [P, R_HC, T])
        quad = sb("quad", [P, 2, T])
        ysum = sb("ysum", [P, T])
        x1 = sb("x1", [P, T])
        xn2 = sb("xn2", [P, T])
        x2T = sb("x2T", [P, T])
        hid = sb("hid", [P, HF, T])
        x3T = [sb(f"x3T{k}", [P, T], FP32R) for k in range(2)]
        rmax = sb("rmax", [P, NT])
        rlog = sb("rlog", [P, NT, NE])
        rexp = sb("rexp", [P, NT, NE])
        rsum = sb("rsum", [P, NT])
        pdif = sb("pdif", [P, NT, NE, NE])
        rank = sb("rank", [P, NT, NE])
        topp = sb("topp", [P, NT, NE])
        tsum = sb("tsum", [P, NT])
        tsafe = sb("tsafe", [P, NT])
        tinv = sb("tinv", [P, NT])
        hm = sb("hm", [P, 2 * FE, T])
        ym = sb("ym", [P, 2, T])
        convb = ym[:, :, :].rearrange("p a (k e) -> p (a k) e", e=D)
        convf = hm[:, 0:KC * D // T, :].rearrange("p a (k e) -> p (a k) e", e=D)
        m1w = hid[:, :, :].rearrange("p k (e f) -> p (k e) f", f=FE * P)

        def bank(name):
            return ctx.enter_context(nc.psum_tensor(name, [P, T], FP32))
        pBC = [bank(f"pBC{k}") for k in range(3)]
        pG = [bank("pG0"), bank("pG1")]
        pH = [bank("pH0"), bank("pH1")]
        pO = bank("pO")

        w_loaded, x0_loaded, xr_loaded, wb_loaded = sem("w_loaded"), sem("x0_loaded"), sem("xr_loaded"), sem("wb_loaded")
        consts_set, expA_done, negA_done, convw_done = sem("consts_set"), sem("expA_done"), sem("negA_done"), sem("convw_done")
        deltaw_mm, deltaw_done = sem("deltaw_mm"), sem("deltaw_done")
        stats_done = [sem(f"stats_done{k}") for k in range(4)]
        mv_done = [sem(f"mv_done{k}") for k in range(4)]
        vare_done = [sem(f"vare_done{k}") for k in range(4)]
        rstd_done = [sem(f"rstd_done{k}") for k in range(4)]
        norm_done = [sem(f"norm_done{k}") for k in range(4)]
        t1_mm, xnfull_done, xnhi_done, xnlo_done, conv_mm, xc_done = (
            sem("t1_mm"), sem("xnfull_done"), sem("xnhi_done"), sem("xnlo_done"), sem("conv_mm"), sem("xc_done"))
        convf_done, zw_split = sem("convf_done"), sem("zw_split")
        z_mm, zs_done, bc_mm, bchi_done = sem("z_mm"), sem("zs_done"), sem("bc_mm"), sem("bchi_done")
        resid_done, midp_done, bc_done = sem("resid_done"), sem("midp_done"), sem("bc_done")
        delta_mm, delta_read, expd_done, lnd_done = sem("delta_mm"), sem("delta_read"), sem("expd_done"), sem("lnd_done")
        onepd_done, limit_done, g_done, glim_done, relu_e_done, delta_done, u_done = (
            sem("onepd_done"), sem("limit_done"), sem("g_done"), sem("glim_done"), sem("relu_e_done"),
            sem("delta_done"), sem("u_done"))
        B_mm, C_mm, cs_done, dA_done, dBx_done = sem("B_mm"), sem("C_mm"), sem("cs_done"), sem("dA_done"), sem("dBx_done")
        scan_done, hC_done, quad_done, quarter_done, ysum_done = (
            sem("scan_done"), sem("hC_done"), sem("quad_done"), sem("quarter_done"), sem("ysum_done"))
        yg_done, out_mm, x1_done, xb_done, xx_done = sem("yg_done"), sem("out_mm"), sem("x1_done"), sem("xb_done"), sem("xx_done")
        t2_mm, x2T_done, hid_mm, hid_done, ffn_mm, res_done = (
            sem("t2_mm"), sem("x2T_done"), sem("hid_mm"), sem("hid_done"), sem("ffn_mm"), sem("res_done"))
        t3_mm, x3hi_done, x3T_done = sem("t3_mm"), sem("x3hi_done"), sem("x3T_done")
        m1w_split, rw_split = sem("m1w_split"), sem("rw_split")
        router_mm, rlog_done, rexp_done, rchain, cw_done = (
            sem("router_mm"), sem("rlog_done"), sem("rexp_done"), sem("rchain"), sem("cw_done"))
        ehid_mm, silu_done, eout_mm, ym_done, acc_done = (
            sem("ehid_mm"), sem("silu_done"), sem("eout_mm"), sem("ym_done"), sem("acc_done"))
        stored = sem("stored")
        parted = {e.engine: sem(f"parted{k}") for k, e in enumerate((nc.scalar, nc.vector, nc.gpsimd))}

        def of(t, b, n=T):
            places = t.shape[1] // n
            return t[:, bass.ds((b if places == NB else b % places) * n, n)]

        def tok(ap, j):
            return ap[:, j * D:(j + 1) * D]

        def apart(engine):
            engine.sem_inc(parted[engine.engine], 1)

        def B_bank(n):
            return pBC[2 * n % 3 if n < NS - 1 else 2]

        def C_bank(n):
            return pBC[(2 * n + 1) % 3 if n != NS - 2 else 0]

        def state_at(st, m):
            return (st[SCAN], m) if m < NS else (st[FRONT], m - NS)

        def slot_in(st, busy, idle):
            return busy if st[SCAN] is not None else idle

        FRONT_LOADS = 9
        BACK_LOADS = 7
        block = ctx.enter_context(nc.Block())

        xv = x.rearrange("b (j p) d -> p b j d", p=P)
        ov = out.rearrange("b (j p) d -> p b j d", p=P)
        xs4 = xs[:, :].rearrange("p (b j d) -> p b j d", b=NB, j=NT)

        @block.sync
        def _(sp):
            sp.dma_start(xs4[:, 0], xv[:, 0]).then_inc(x0_loaded, 16)
            sp.dma_start(vec[:, :], vecs).then_inc(w_loaded, 16)
            sp.dma_start(ident[:, :], identity).then_inc(w_loaded, 16)
            sp.dma_start(inw[:, :], in_wT).then_inc(w_loaded, 16)
            sp.dma_start(convb, conv_rows.unsqueeze(0).broadcast_to([P, KC, D])).then_inc(w_loaded, 16)
            sp.dma_start(xbcw[:, :], xbc_wT).then_inc(w_loaded, 16)
            sp.dma_start(xdtw[:, :], xdt_w).then_inc(w_loaded, 16)
            sp.dma_start(dtw[:, :], dt_wT).then_inc(w_loaded, 16)
            sp.dma_start(sel[:, :], select).then_inc(w_loaded, 16)
            sp.dma_start(tie[:, :], tie_limit).then_inc(w_loaded, 16)
            sp.dma_start(xs4[:, 1:NB], xv[:, 1:NB]).then_inc(xr_loaded, 16)
            sp.dma_start(outw[:, :], out_wT).then_inc(wb_loaded, 16)
            sp.dma_start(f1w[:, :], w1T).then_inc(wb_loaded, 16)
            sp.dma_start(f2w[:, :, :], w2T).then_inc(wb_loaded, 16)
            sp.dma_start(b2all[:, :], b2.broadcast_to([P, D])).then_inc(wb_loaded, 16)
            sp.dma_start(rw[:, :], router_w).then_inc(wb_loaded, 16)
            sp.dma_start(m1w, moe_w1).then_inc(wb_loaded, 16)
            sp.dma_start(m2w[:, :, :, :], moe_w2).then_inc(wb_loaded, 16)
            with sp.Fori(0, NB) as b:
                sp.wait_ge(acc_done, b * NE + NE)
                sp.dma_start(ov[:, bass.ds(b, 1)], xs4[:, bass.ds(b, 1)]).then_inc(stored, 16)
            sp.wait_ge(stored, 16 * NB)

        HIDDEN_AT = [2, 4, 6, 8, 10, 12, 14, 16]
        SILU_AT = [3, 5, 7, 9, 11, 13, 15, 17]
        OUT_AT = [5, 7, 9, 11, 13, 15, 17, 19]
        WEIGH_AT = [6, 8, 10, 12, 14, 16, 18, 20]

        CONV_AT = (14, 14, 14, 15, 15, 16, 16, 16)
        FFN_AT = (12, 12, 13, 13)
        BANK = dict(t1=0, conv=0, bc=0, delta=0, z=0, h3=0, t3=1, router=1, out=1, t2=1, h0=1, h1=1, h2=1, ffn=1)

        def z_bank(st):
            return slot_in(st, BANK["z"], 1 - BANK["z"])

        def experts_at(slots, n, st):
            for e, slot in enumerate(slots):
                if slot < NS and slot == n and st[EXPERT] is not None:
                    yield st[EXPERT], e
                if slot >= NS and slot - NS == n and st[TAIL] is not None:
                    yield st[TAIL], e

        @block.tensor
        def _(pe):
            turns = [("t3", (1,), EXPERT, 1, x3T_done, 1, 1), ("out", (2,), MIDDLE, 1, x1_done, 1, 1),
                     ("delta", (3,), FRONT, 0, delta_read, 1, 1), ("router", (4,), EXPERT, 1, rlog_done, 1, 1),
                     ("z", (5,), FRONT, 0, zs_done, 1, 1), ("t2", (6,), MIDDLE, 1, x2T_done, 1, 1),
                     ("bc", (7,), FRONT, 0, resid_done, 1, 1), ("h0", (7,), MIDDLE, 1, hid_done, HF, 1),
                     ("h1", (8,), MIDDLE, 1, hid_done, HF, 2), ("h2", (9,), MIDDLE, 1, hid_done, HF, 3),
                     ("h3", (10,), MIDDLE, 0, hid_done, HF, 4), ("ffn", FFN_AT, MIDDLE, 1, res_done, 1, 1),
                     ("t1", (12,), NORMS, 0, xnfull_done, 1, 1), ("conv", CONV_AT, NORMS, 0, xc_done, 1, 1)]
            assert [(t[0], t[3]) for t in turns if t[3] != BANK[t[0]]] == []

            def bank_of(st, k):
                return z_bank(st) if turns[k][0] == "z" else turns[k][3]

            def wait_bank(i, k):
                for back in range(1, 2 * len(turns)):
                    j = k - back
                    r = i if j >= 0 else i - 1
                    if isinstance(r, int) and r < FIRST_ROUND:
                        return
                    _, _, stage, _, read, per, nth = turns[j % len(turns)]
                    b = stages(r)[stage]
                    if bank_of(stages(r), j % len(turns)) == bank_of(stages(i), k) and b is not None:
                        pe.wait_ge(read, b * per + nth)
                        return

            def transpose4(dst, src, done):
                for j in range(NT):
                    last = nc.tensor.transpose(tok(dst, j), tok(src, j), ident[:, :])
                last.then_inc(done, 1)

            pe.wait_ge(w_loaded, 16 * FRONT_LOADS)
            nc.tensor.matmul(pG[0][:, 0:D], xdtw[:, :], dtw[:, :], start=True, stop=True).then_inc(deltaw_mm, 1)
            pe.wait_ge(deltaw_done, 1)

            def product(st, name, b, part):
                pg = pG[z_bank(st) if name == "z" else BANK[name]]
                if name == "router":
                    pe.wait_ge(x3T_done, b + 1)
                    if isinstance(b, int) and b == 0:
                        pe.wait_ge(rw_split, 2)
                    for j in range(NT):
                        for k, (a, w) in enumerate(((0, 0), (0, 1), (1, 0))):
                            last = nc.tensor.matmul(pg[:, j * NE:(j + 1) * NE], x3T[a][:, j * P:(j + 1) * P],
                                                    rwp[w][:, :], start=(k == 0), stop=(k == 2))
                    last.then_inc(router_mm, 1)
                elif name == "out":
                    pe.wait_ge(yg_done, b + 1)
                    for j in range(NT):
                        last = nc.tensor.matmul(tok(pg, j), ysum[:, j * P:(j + 1) * P], outw[:, :], start=True, stop=True)
                    last.then_inc(out_mm, 1)
                elif name == "t1":
                    pe.wait_ge(norm_done[1], b + 1)
                    transpose4(pg, xn1, t1_mm)
                elif name == "t2":
                    pe.wait_ge(norm_done[2], b + 1)
                    transpose4(pg, xn2, t2_mm)
                elif name == "t3":
                    pe.wait_ge(norm_done[3], b + 1)
                    transpose4(pg, xn2, t3_mm)
                elif name == "conv":
                    if part == 0:
                        pe.wait_ge(xnhi_done, b + 1)
                        if isinstance(b, int) and b == 0:
                            pe.wait_ge(convw_done, 2)
                    for k, (w, a) in enumerate(((0, 0), (1, 0), (0, 1))):
                        if part == 0 and k == 2:
                            pe.wait_ge(xnlo_done, b + 1)
                        last = nc.tensor.matmul(pg[:, :], convw[w][:, part, :], xnT[a][:, part:part + T],
                                                start=(part == 0 and k == 0), stop=(part == KC - 1 and k == 2))
                    if part == KC - 1:
                        last.then_inc(conv_mm, 1)
                elif name == "z":
                    if isinstance(b, int) and b == 0:
                        pe.wait_ge(zw_split, 2)
                    for k, (w, a) in enumerate(((0, 0), (1, 0), (0, 1))):
                        last = nc.tensor.matmul(pg[:, :], zw[w][:, :], xnT[a][:, KC - 1:], start=(k == 0), stop=(k == 2))
                    last.then_inc(z_mm, 1)
                elif name == "bc":
                    nc.tensor.matmul(pg[0:BCP, :], xbcw[:, :], of(xc, b), start=True, stop=True).then_inc(bc_mm, 1)
                elif name == "delta":
                    pe.wait_ge(xc_done, b + 1)
                    nc.tensor.matmul(pg[:, :], deltaw[:, :], of(xc, b), start=True, stop=True).then_inc(delta_mm, 1)
                elif name == "ffn":
                    if part == 0:
                        pe.wait_ge(hid_done, HF * b + HF)
                    for k in range(HF):
                        last = nc.tensor.matmul(tok(pg, part), hid[:, k, part * P:(part + 1) * P], f2w[:, k, :],
                                                start=(k == 0), stop=(k == HF - 1))
                    if part == NT - 1:
                        last.then_inc(ffn_mm, 1)
                else:
                    k = int(name[1])
                    if k == 0:
                        pe.wait_ge(x2T_done, b + 1)
                    nc.tensor.matmul(pg[:, :], f1w[:, k * P:(k + 1) * P], x2T[:, :], start=True, stop=True).then_inc(hid_mm, 1)

            def broadcast(row, bank, b, done):
                nc.tensor.matmul(bank[:, :], sel[:, row:row + 1].broadcast_to([BCP, P]), of(bc, b), start=True, stop=True).then_inc(done, 1)

            def broadcast_B(b, n):
                later = not isinstance(b, int) or b >= 1
                if n == 0:
                    pe.wait_ge(bc_done, 2 * b + 2)
                    if later:
                        pe.wait_ge(cs_done, b * NS - 1)
                elif n == 1:
                    if later:
                        pe.wait_ge(dBx_done, b * NS)
                elif n == NS - 1:
                    pe.wait_ge(dBx_done, b * NS + n - 1)
                else:
                    pe.wait_ge(cs_done, b * NS + n - 1)
                broadcast(n, B_bank(n), b, B_mm)

            def broadcast_C(b, n):
                if n == 0:
                    if not isinstance(b, int) or b >= 1:
                        pe.wait_ge(cs_done, b * NS)
                elif n == NS - 2:
                    pe.wait_ge(cs_done, b * NS + n)
                else:
                    pe.wait_ge(dBx_done, b * NS + n)
                broadcast(NS + n, C_bank(n), b, C_mm)

            def expert_hidden(b, e):
                if e == 0:
                    pe.wait_ge(x3T_done, b + 1)
                    if isinstance(b, int) and b == 0:
                        pe.wait_ge(m1w_split, 2)
                for f in range(FE):
                    if not isinstance(b, int) or b * NE + e >= 1:
                        pe.wait_ge(silu_done, b * NE * FE + e * FE + f - 1)
                    for k, (w, a) in enumerate(((0, 0), (1, 0), (0, 1))):
                        last = nc.tensor.matmul(pH[f][:, :], m1wp[w][:, e, f * P:(f + 1) * P], x3T[a][:, :],
                                                start=(k == 0), stop=(k == 2))
                    last.then_inc(ehid_mm, 1)

            def expert_out(b, e):
                pe.wait_ge(silu_done, b * NE * FE + e * FE + 2)
                if not isinstance(b, int) or b * NE + e >= 1:
                    pe.wait_ge(ym_done, b * NE + e)
                for j in range(NT):
                    for f in range(FE):
                        last = nc.tensor.matmul(tok(pO, j), hm[:, (e % 2) * FE + f, j * P:(j + 1) * P], m2w[:, e, f, :],
                                                start=(f == 0), stop=(f == FE - 1))
                last.then_inc(eout_mm, 1)

            def experts(st, n):
                for b, e in experts_at(HIDDEN_AT, n, st):
                    expert_hidden(b, e)
                for b, e in experts_at(OUT_AT, n, st):
                    expert_out(b, e)

            def body(i):
                st = stages(i)
                if isinstance(i, int) and i == 1:
                    pe.wait_ge(wb_loaded, 16 * BACK_LOADS)
                for n in range(NS):
                    b, m = state_at(st, n + 1)
                    if b is not None:
                        broadcast_C(b, m)
                    b, m = state_at(st, n + 2)
                    if b is not None:
                        broadcast_B(b, m)
                    if st[SCAN] is None and n == 2:
                        experts(st, n)
                    for k, (name, slots, stage, *_) in enumerate(turns):
                        for part, slot in enumerate(slots):
                            b = st[stage] if slot < NS else st[stage + 1]
                            if slot % NS == n and b is not None:
                                if part == 0:
                                    wait_bank(i, k)
                                product(st, name, b, part)
                    if not (st[SCAN] is None and n == 2):
                        experts(st, n)

            rounds(pe, body)

        @block.scalar
        def _(act):
            act.wait_ge(w_loaded, 16 * FRONT_LOADS)
            nc.scalar.activation(expA[:, :], vec[:, V_ALOG:V_ALOG + NS], ACT.Exp).then_inc(expA_done, 1)
            act.wait_ge(deltaw_mm, 1)
            nc.scalar.activation(deltaw[:, :], pG[0][:, 0:D], ACT.Copy).then_inc(deltaw_done, 1)

            DECAYS_AFTER = {13: (16, 17, 18)}

            def decays_before(i):
                if isinstance(i, int) and i == NB - 2:
                    return {4: (12, 13), 5: (14, 15), 14: (19, 20, 21), 15: (22, 23)}
                if isinstance(i, int) and i == NB - 1:
                    return {4: (8, 9, 10), 5: (11, 12), 10: (13, 14, 15)}
                return {4: (12, 13), 5: (14, 15), 14: (19, 20, 21, 22, 23), 15: (24, 25, 26, 27)}

            def decay(b, n):
                if n == 0:
                    act.wait_ge(delta_done, b + 1)
                    if isinstance(b, int) and b == 0:
                        act.wait_ge(negA_done, 1)
                if not isinstance(b, int) or b >= 1:
                    act.wait_ge(scan_done, (b - 1) * NS + n + 1)
                apart(act)
                nc.scalar.activation(dA[:, n, :], of(delta, b), ACT.Exp,
                                     scale=negA[:, n:n + 1]).then_inc(dA_done, 1)

            def body(i):
                st = stages(i)
                norms, front, middle, expert = st[NORMS], st[FRONT], st[MIDDLE], st[EXPERT]
                for n in range(NS):
                    b, m = state_at(st, n + 1)
                    if b is not None:
                        act.wait_ge(C_mm, b * NS + m + 1)
                        if not isinstance(b, int) or NS * b + m >= R_H:
                            act.wait_ge(hC_done, b * NS + m - R_H + 1)
                        nc.scalar.activation(cs[:, m % R_H, :], C_bank(m)[:, :], ACT.Copy).then_inc(cs_done, 1)
                    if norms is not None and n == 12:
                        act.wait_ge(t1_mm, norms + 1)
                        nc.scalar.activation(xn1[:, :], pG[BANK["t1"]][:, :], ACT.Identity,
                                             scale=vec[:, V_G1:V_G1 + 1], bias=vec[:, V_B1:V_B1 + 1]).then_inc(xnfull_done, 1)
                        if isinstance(norms, int) and norms == 0:
                            act.wait_ge(consts_set, 1)
                        else:
                            act.wait_ge(z_mm, norms)
                            act.wait_ge(conv_mm, norms)
                        act.wait_ge(xnfull_done, norms + 1)
                        nc.scalar.activation(xnT[0][:, KC - 1:], xn1[:, :], ACT.Copy).then_inc(xnhi_done, 1)
                    if expert is not None and n == 1:
                        act.wait_ge(t3_mm, expert + 1)
                        if not isinstance(expert, int) or expert >= 1:
                            act.wait_ge(ehid_mm, expert * NE * FE)
                        nc.scalar.activation(x3T[0][:, :], pG[BANK["t3"]][:, :], ACT.Copy).then_inc(x3hi_done, 1)
                    if front is not None and n == 2:
                        act.wait_ge(conv_mm, front + 1)
                        if not isinstance(front, int) or front >= 2:
                            act.wait_ge(ysum_done, 4 * front - 7)
                            act.wait_ge(u_done, front - 1)
                            act.wait_ge(delta_mm, front - 1)
                            act.wait_ge(bc_mm, front - 1)
                        apart(act)
                        nc.scalar.activation(of(xc, front), pG[BANK["conv"]][:, :], ACT.Silu,
                                             bias=vec[:, V_CONVB:V_CONVB + 1]).then_inc(xc_done, 1)
                    if front is not None and n == slot_in(st, 6, 8):
                        act.wait_ge(z_mm, front + 1)
                        if not isinstance(front, int) or front >= 2:
                            act.wait_ge(yg_done, front - 1)
                        apart(act)
                        nc.scalar.activation(of(zs, front), pG[z_bank(st)][:, :], ACT.Silu).then_inc(zs_done, 1)
                    if front is not None and n == 7:
                        act.wait_ge(bc_mm, front + 1)
                        apart(act)
                        nc.scalar.activation(of(bc, front), pG[BANK["bc"]][0:BCP, :], ACT.Copy).then_inc(bchi_done, 1)
                    if front is not None and n == 3:
                        bias = vec[:, V_DTB:V_DTB + 1]
                        act.wait_ge(delta_mm, front + 1)
                        nc.scalar.activation(expd[:, :], pG[BANK["delta"]][:, :], ACT.Abs, bias=bias)
                        nc.scalar.activation(reld[:, :], pG[BANK["delta"]][:, :], ACT.Relu, bias=bias).then_inc(delta_read, 1)
                    if middle is not None and n == 6:
                        act.wait_ge(t2_mm, middle + 1)
                        nc.scalar.activation(x2T[:, :], pG[BANK["t2"]][:, :], ACT.Identity, scale=vec[:, V_G2:V_G2 + 1],
                                             bias=vec[:, V_B2:V_B2 + 1]).then_inc(x2T_done, 1)
                    if front is not None and n == 4:
                        act.wait_ge(delta_read, front + 1)
                        nc.scalar.activation(expd[:, :], expd[:, :], ACT.Exp, scale=-1.0).then_inc(expd_done, 1)
                    if front is not None and n == slot_in(st, 8, 4):
                        act.wait_ge(expd_done, front + 1)
                        nc.scalar.activation(lnd[:, :], expd[:, :], ACT.Ln, bias=1.0).then_inc(lnd_done, 1)
                    if expert is not None and n == 5:
                        act.wait_ge(rlog_done, expert + 1)
                        nc.scalar.activation(rexp[:, :, :], rlog[:, :, :], ACT.Exp).then_inc(rexp_done, 1)
                    for m in decays_before(i).get(n, ()):
                        b, m = state_at(st, m)
                        if b is not None:
                            decay(b, m)
                    for b, e in experts_at(SILU_AT, n, st):
                        for f in range(FE):
                            act.wait_ge(ehid_mm, b * NE * FE + e * FE + f + 1)
                            if not isinstance(b, int) or b * NE + e >= 2:
                                act.wait_ge(eout_mm, b * NE + e - 1)
                            nc.scalar.activation(hm[:, (e % 2) * FE + f, :], pH[f][:, :], ACT.Silu).then_inc(silu_done, 1)
                    if middle is not None and 7 <= n < 7 + HF:
                        k = n - 7
                        act.wait_ge(hid_mm, middle * HF + k + 1)
                        if isinstance(middle, int) and middle == 0:
                            act.wait_ge(m1w_split, 2)
                        nc.scalar.activation(hid[:, k, :], pG[BANK[f"h{k}"]][:, :], ACT.Relu,
                                             bias=vec[:, V_FB + k:V_FB + k + 1]).then_inc(hid_done, 1)
                    if front is not None and n == 10:
                        act.wait_ge(resid_done, front + 1)
                        nc.scalar.activation(midp[64:96, :], resid[64:96, :], ACT.Copy).then_inc(midp_done, 1)
                        apart(act)
                        nc.scalar.activation(bc[32:64, bass.ds(front % 2 * T, T)], resid[32:64, :], ACT.Copy).then_inc(bc_done, 1)
                    for m in DECAYS_AFTER.get(n, ()):
                        b, m = state_at(st, m)
                        if b is not None:
                            decay(b, m)

            rounds(act, body)

        @block.vector
        def _(dve):
            for part in xnT:
                nc.vector.memset(part[:, 0:KC - 1].bitcast(FP32), 0.0)
            nc.vector.memset(neghalf[:, :], -0.5).then_inc(consts_set, 1)

            def split(parts, whole, done):
                nc.vector.tensor_copy(parts[0], whole).then_inc(done, 1)
                dve.wait_ge(done, 1)
                nc.vector.tensor_tensor(parts[1], whole, parts[0].bitcast(FP32), ALU.subtract).then_inc(done, 1)

            def statistics(k, b, src):
                apart(dve)
                for j in range(NT):
                    last = nc.vector.bn_stats(stat[k][:, j, :], tok(src, j))
                last.then_inc(stats_done[k], 1)

            def gather(k, b):
                dve.wait_ge(stats_done[k], b + 1)
                apart(dve)
                for j in range(NT):
                    last = nc.vector.bn_aggr(mv[k][:, j, :], stat[k][:, j, :])
                last.then_inc(mv_done[k], 1)

            def normalise(k, b, dst, src):
                dve.wait_ge(rstd_done[k], b + 1)
                apart(dve)
                for j in range(NT):
                    last = nc.vector.tensor_scalar(tok(dst, j), tok(src, j), mv[k][:, j, 0:1], rstd[k][:, j:j + 1],
                                                   ALU.subtract, ALU.mult)
                last.then_inc(norm_done[k], 1)

            def drive(b, n):
                if n == 0:
                    dve.wait_ge(u_done, b + 1)
                dve.wait_ge(B_mm, b * NS + n + 1)
                if not isinstance(b, int) or NS * b + n >= R_DBX:
                    dve.wait_ge(scan_done, b * NS + n - R_DBX + 1)
                nc.vector.tensor_tensor(dBx[:, n % R_DBX, :], of(u, b), B_bank(n)[:, :], ALU.mult).then_inc(dBx_done, 1)

            SUM_AT = (7, 11, 13)

            def sum_pairs(b, q):
                a = 4 * q % R_HC
                dve.wait_ge(hC_done, b * NS + 4 * q + 4)
                if not isinstance(b, int) or 4 * b + q >= 1:
                    dve.wait_ge(ysum_done, 4 * b + q)
                nc.vector.tensor_tensor(quad[:, :, :], hC[:, a:a + 2, :], hC[:, a + 2:a + 4, :], ALU.add).then_inc(quad_done, 1)

            def sum_quad(b, q):
                dve.wait_ge(quad_done, 4 * b + q + 1)
                nc.vector.tensor_tensor(quad[:, 0, :], quad[:, 0, :], quad[:, 1, :], ALU.add).then_inc(quarter_done, 1)

            def sum_total(b, q):
                dve.wait_ge(quarter_done, 4 * b + q + 1)
                if q == 0:
                    if not isinstance(b, int) or b >= 1:
                        dve.wait_ge(out_mm, b)
                    nc.vector.scalar_tensor_tensor(out=ysum[:, :], in0=of(xc, b), scalar=vec[:, V_D:V_D + 1],
                                                   in1=quad[:, 0, :], op0=ALU.mult, op1=ALU.add).then_inc(ysum_done, 1)
                else:
                    nc.vector.tensor_tensor(ysum[:, :], ysum[:, :], quad[:, 0, :],
                                            ALU.add).then_inc(ysum_done, 1)

            def router_head(b):
                dve.wait_ge(router_mm, b + 1)
                logits = pG[BANK["router"]][:, 0:NT * NE].rearrange("p (j e) -> p j e", j=NT)
                nc.vector.tensor_reduce(rmax[:, :], logits, AX.X, ALU.max).then_inc(rchain, 1)
                dve.wait_ge(rchain, R_CHAIN * b + 1)
                nc.vector.tensor_tensor(rlog[:, :, :], logits, rmax[:, :].unsqueeze(2).broadcast_to([P, NT, NE]),
                                        ALU.subtract).then_inc(rlog_done, 1)

            def router_tail(b):
                count = [1]

                def link(op):
                    count[0] += 1
                    op.then_inc(rchain, 1)
                    dve.wait_ge(rchain, R_CHAIN * b + count[0])

                def over_experts(t):
                    return t[:, :].unsqueeze(2).broadcast_to([P, NT, NE])

                dve.wait_ge(rexp_done, b + 1)
                link(nc.vector.tensor_tensor(pdif[:, :, :, :], rexp[:, :, :].unsqueeze(2).broadcast_to([P, NT, NE, NE]),
                                             rexp[:, :, :].unsqueeze(3).broadcast_to([P, NT, NE, NE]), ALU.subtract))
                before = pdif[:, :, :, :].rearrange("p t e j -> p t (e j)")
                link(nc.vector.tensor_tensor(before, before,
                                             tie[:, :].unsqueeze(1).broadcast_to([P, NT, NE * NE]), ALU.is_ge))
                nc.vector.tensor_reduce(rsum[:, :], rexp[:, :, :], AX.X, ALU.add)
                link(nc.vector.tensor_reduce(rank[:, :, :], pdif[:, :, :, :],
                                             AX.X, ALU.add))
                link(nc.vector.scalar_tensor_tensor(out=topp[:, :, :], in0=rank[:, :, :], scalar=2.0, in1=rexp[:, :, :],
                                                    op0=ALU.is_lt, op1=ALU.mult))
                link(nc.vector.tensor_reduce(tsum[:, :], topp[:, :, :], AX.X, ALU.add))
                link(nc.vector.scalar_tensor_tensor(out=tsafe[:, :], in0=rsum[:, :], scalar=EPS_TOP, in1=tsum[:, :],
                                                    op0=ALU.mult, op1=ALU.max))
                link(nc.vector.reciprocal(tinv[:, :], tsafe[:, :]))
                assert count[0] == R_CHAIN
                nc.vector.tensor_tensor(of(cw, b, NT * NE).rearrange("p (j e) -> p j e", j=NT), topp[:, :, :],
                                        over_experts(tinv), ALU.mult).then_inc(cw_done, 1)

            def weigh(b, e):
                dve.wait_ge(eout_mm, b * NE + e + 1)
                if e == 0:
                    dve.wait_ge(cw_done, b + 1)
                if not isinstance(b, int) or b * NE + e >= 2:
                    dve.wait_ge(acc_done, b * NE + e - 1)
                w = of(cw, b, NT * NE).rearrange("p (j e) -> p j e", j=NT)[:, :, e:e + 1].broadcast_to([P, NT, D])
                nc.vector.tensor_tensor(ym[:, e % 2, :].rearrange("p (j d) -> p j d", j=NT),
                                        pO[:, :].rearrange("p (j d) -> p j d", j=NT), w, ALU.mult).then_inc(ym_done, 1)

            def body(i):
                st = stages(i)
                norms, front, scan, middle, expert = st[:TAIL]
                for n in range(NS):
                    b, m = state_at(st, n + 1)
                    if b is not None:
                        drive(b, m)
                    if scan is not None and n - 1 in SUM_AT:
                        sum_quad(scan, SUM_AT.index(n - 1))
                    if middle is not None and n == 3:
                        dve.wait_ge(x1_done, middle + 1)
                        statistics(2, middle, x1)
                    if norms is not None and n == 4:
                        gather(0, norms)
                    if norms is not None and n == slot_in(st, 9, 5):
                        dve.wait_ge(norm_done[0], norms + 1)
                        statistics(1, norms, of(xa, norms))
                    if middle is not None and n == 15:
                        gather(3, middle)
                    if scan is not None:
                        dve.wait_ge(dBx_done, scan * NS + n + 1)
                        dve.wait_ge(dA_done, scan * NS + n + 1)
                        if not isinstance(scan, int) or NS * scan + n >= R_H:
                            dve.wait_ge(hC_done, scan * NS + n - R_H + 1)
                        nc.vector.tensor_tensor_scan(hs[:, n % R_H, :], dA[:, n, :], dBx[:, n % R_DBX, :], 0.0,
                                                     ALU.mult, ALU.add).then_inc(scan_done, 1)
                    if middle is not None and n == 3:
                        gather(2, middle)
                    if norms is not None and n == slot_in(st, 9, 5):
                        gather(1, norms)
                    if scan is not None and n - 1 in SUM_AT:
                        sum_total(scan, SUM_AT.index(n - 1))
                    if n == 5 and expert is not None:
                        router_tail(expert)
                    if n == 8 and front is not None:
                        dve.wait_ge(bchi_done, front + 1)
                        nc.vector.tensor_tensor(resid[:, :], pG[BANK["bc"]][0:BCP, :], of(bc, front),
                                                ALU.subtract).then_inc(resid_done, 1)
                    for b, e in experts_at(WEIGH_AT, n, st):
                        weigh(b, e)
                    if n == 0 and middle is not None:
                        sum_pairs(middle, 3)
                        sum_quad(middle, 3)
                        sum_total(middle, 3)
                    if n == 1 and expert is not None:
                        dve.wait_ge(x3hi_done, expert + 1)
                        nc.vector.tensor_tensor(x3T[1][:, :], pG[BANK["t3"]][:, :], x3T[0][:, :].bitcast(FP32),
                                                ALU.subtract).then_inc(x3T_done, 1)
                    if n == 2 and middle is not None:
                        dve.wait_ge(out_mm, middle + 1)
                        if not isinstance(middle, int) or middle >= 1:
                            dve.wait_ge(xx_done, middle)
                        nc.vector.tensor_tensor(x1[:, :], of(xa, middle), pG[BANK["out"]][:, :], ALU.add).then_inc(x1_done, 1)
                    if n == 4:
                        if middle is not None:
                            if not isinstance(middle, int) or middle >= 1:
                                dve.wait_ge(t3_mm, middle)
                            normalise(2, middle, xn2, x1)
                        if expert is not None:
                            router_head(expert)
                    if n == slot_in(st, 8, 5) and front is not None:
                        dve.wait_ge(expd_done, front + 1)
                        apart(dve)
                        nc.vector.tensor_scalar(of(delta, front), expd[:, :], 1.0, None, ALU.add).then_inc(onepd_done, 1)
                    if n == 11 and front is not None:
                        dve.wait_ge(midp_done, front + 1)
                        nc.vector.tensor_tensor(bc[64:96, bass.ds(front % 2 * T, T)], resid[64:96, :], midp[64:96, :],
                                                ALU.subtract).then_inc(bc_done, 1)
                    if n == slot_in(st, 9, 5) and front is not None:
                        dve.wait_ge(onepd_done, front + 1)
                        dve.wait_ge(lnd_done, front + 1)
                        nc.vector.scalar_tensor_tensor(out=lnd[:, :], in0=of(delta, front), scalar=-1.0, in1=lnd[:, :],
                                                       op0=ALU.add, op1=ALU.subtract).then_inc(g_done, 1)
                        dve.wait_ge(g_done, front + 1)
                        dve.wait_ge(limit_done, front + 1)
                        nc.vector.scalar_tensor_tensor(out=lnd[:, :], in0=lnd[:, :], scalar=0.0, in1=of(u, front),
                                                       op0=ALU.max, op1=ALU.min).then_inc(glim_done, 1)
                    if n == 3 and norms is not None:
                        if isinstance(i, int) and i == FIRST_ROUND:
                            dve.wait_ge(x0_loaded, 16)
                        if isinstance(i, int) and i == FIRST_ROUND + 1:
                            dve.wait_ge(xr_loaded, 16)
                        statistics(0, norms, of(xs, norms))
                    if isinstance(i, int) and i == FIRST_ROUND + 1 and n == 12:
                        dve.wait_ge(expA_done, 1)
                        nc.vector.tensor_scalar(negA[:, :], expA[:, :], -1.0, None, ALU.mult).then_inc(negA_done, 1)
                        dve.wait_ge(wb_loaded, 16 * BACK_LOADS)
                        split([w[:, :] for w in rwp], rw[:, :], rw_split)
                        split([w[:, :, :] for w in m1wp], m1w, m1w_split)
                    if n == slot_in(st, 8, 4) and norms is not None:
                        normalise(0, norms, of(xa, norms), of(xs, norms))
                    if n == slot_in(st, 11, 6) and norms is not None:
                        if not isinstance(norms, int) or norms >= 1:
                            dve.wait_ge(xnhi_done, norms)
                            dve.wait_ge(xnlo_done, norms)
                        normalise(1, norms, xn1, of(xa, norms))
                        if isinstance(i, int) and i == FIRST_ROUND:
                            dve.wait_ge(convf_done, 1)
                            split([w[:, :, :] for w in convw], convf, convw_done)
                            split([w[:, :] for w in zw], inw[:, D:2 * D], zw_split)
                    if n == 14 and middle is not None:
                        dve.wait_ge(ffn_mm, middle + 1)
                        dve.wait_ge(xx_done, middle + 1)
                        nc.vector.tensor_tensor(of(xs, middle), of(xs, middle), pG[BANK["ffn"]][:, :], ALU.add).then_inc(res_done, 1)
                        dve.wait_ge(res_done, middle + 1)
                        statistics(3, middle, of(xs, middle))
                    if scan is not None and n in SUM_AT:
                        sum_pairs(scan, SUM_AT.index(n))
                    if n == 15 and middle is not None:
                        dve.wait_ge(t2_mm, middle + 1)
                        normalise(3, middle, xn2, of(xs, middle))
            rounds(dve, body)

        @block.gpsimd
        def _(pool):
            pool.wait_ge(consts_set, 1)

            def inverse_deviation(k, b):
                pool.wait_ge(mv_done[k], b + 1)
                apart(pool)
                nc.gpsimd.tensor_scalar(vare[k][:, :], mv[k][:, :, 1], EPS_LN, 1.0, ALU.add, ALU.mult).then_inc(vare_done[k], 1)
                pool.wait_ge(vare_done[k], b + 1)
                nc.gpsimd.tensor_tensor(rstd[k][:, :], vare[k][:, :], neghalf[:, :], ALU.pow).then_inc(rstd_done[k], 1)

            def add_expert(b, e):
                pool.wait_ge(ym_done, b * NE + e + 1)
                if not isinstance(b, int) or b * NE + e >= 1:
                    pool.wait_ge(acc_done, b * NE + e)
                apart(pool)
                nc.gpsimd.tensor_tensor(of(xs, b), of(xs, b), ym[:, e % 2, :], ALU.add).then_inc(acc_done, 1)

            def body(i):
                st = stages(i)
                norms, front, scan, middle = st[NORMS], st[FRONT], st[SCAN], st[MIDDLE]
                for n in range(NS):
                    if scan is not None:
                        pool.wait_ge(scan_done, scan * NS + n + 1)
                        pool.wait_ge(cs_done, scan * NS + n + 1)
                        if not isinstance(scan, int) or NS * scan + n >= R_HC:
                            pool.wait_ge(quad_done, 4 * scan + n // 4 - 1)
                        nc.gpsimd.tensor_tensor(hC[:, n % R_HC, :], hs[:, n % R_H, :], cs[:, n % R_H, :],
                                                ALU.mult).then_inc(hC_done, 1)
                    if n == 0 and middle is not None:
                        pool.wait_ge(ysum_done, 4 * middle + 4)
                        apart(pool)
                        nc.gpsimd.tensor_tensor(ysum[:, :], ysum[:, :], of(zs, middle), ALU.mult).then_inc(yg_done, 1)
                    if n == 3 and middle is not None:
                        inverse_deviation(2, middle)
                    if n == 4 and middle is not None:
                        pool.wait_ge(xb_done, middle + 1)
                        apart(pool)
                        nc.gpsimd.tensor_tensor(of(xs, middle), of(xs, middle), x1[:, :], ALU.add).then_inc(xx_done, 1)
                    if n == 11 and front is not None:
                        pool.wait_ge(norm_done[0], front + 1)
                        if isinstance(front, int) and front == 0:
                            pool.wait_ge(wb_loaded, 16 * BACK_LOADS)
                        apart(pool)
                        whole = of(xs, front).rearrange("p (j d) -> p j d", j=NT)
                        nc.gpsimd.tensor_tensor(whole, whole, b2all[:, :].unsqueeze(1).broadcast_to([P, NT, D]),
                                                ALU.add).then_inc(xb_done, 1)
                    if n == 4 and norms is not None:
                        inverse_deviation(0, norms)
                    if n == slot_in(st, 9, 4) and norms is not None:
                        inverse_deviation(1, norms)
                        if isinstance(i, int) and i == FIRST_ROUND:
                            pool.wait_ge(w_loaded, 16 * FRONT_LOADS)
                            nc.gpsimd.tensor_tensor(convf, inw[:, 0:D].unsqueeze(1).broadcast_to([P, KC, D]),
                                                    convb, ALU.mult).then_inc(convf_done, 1)
                    if n == slot_in(st, 7, 5) and front is not None:
                        pool.wait_ge(expd_done, front + 1)
                        apart(pool)
                        nc.gpsimd.tensor_tensor(of(u, front), expd[:, :], expd[:, :], ALU.mult).then_inc(limit_done, 1)
                        nc.gpsimd.tensor_tensor(reld[:, :], reld[:, :], expd[:, :], ALU.add).then_inc(relu_e_done, 1)
                    if n == slot_in(st, 10, 5) and front is not None:
                        pool.wait_ge(glim_done, front + 1)
                        pool.wait_ge(relu_e_done, front + 1)
                        apart(pool)
                        nc.gpsimd.tensor_tensor(of(delta, front), reld[:, :], lnd[:, :], ALU.subtract).then_inc(delta_done, 1)
                        pool.wait_ge(delta_done, front + 1)
                        apart(pool)
                        nc.gpsimd.tensor_tensor(of(u, front), of(delta, front), of(xc, front), ALU.mult).then_inc(u_done, 1)
                    if n == 14 and middle is not None:
                        inverse_deviation(3, middle)
                    for b, e in experts_at(WEIGH_AT, n, st):
                        add_expert(b, e)
                    if n == 12 and norms is not None:
                        pool.wait_ge(xnhi_done, norms + 1)
                        nc.gpsimd.tensor_tensor(xnT[1][:, KC - 1:], xn1[:, :], xnT[0][:, KC - 1:].bitcast(FP32),
                                                ALU.subtract).then_inc(xnlo_done, 1)

            rounds(pool, body)


R_CHAIN = 8


def kernel(**inputs):
    import numpy as np
    import ml_dtypes
    import concourse.bacc as bacc
    from concourse.bass_utils import run_bass_kernel_spmd

    a = {k: np.asarray(v) for k, v in inputs.items()}
    g = lambda name: a["L0_attn_" + name]
    columns = [g("conv_b"), g("dt_proj_b"), g("D_param"), g("ln1_g"), g("ln1_b"), g("ln2_g"), g("ln2_b")]
    columns += list(g("b1").reshape(HF, P))
    xp = g("x_proj_w")
    arrays = dict(
        x=g("x"),
        vecs=np.concatenate([np.stack(columns, axis=1), g("A_log")], axis=1),
        in_wT=g("in_proj_w").T,
        conv_rows=g("conv_w").T,
        xbc_wT=np.concatenate([xp[8:40]] * 3, axis=0).T,
        xdt_w=xp[0:8],
        dt_wT=g("dt_proj_w").T,
        out_wT=g("out_proj_w").T,
        w1T=g("w1").T,
        w2T=g("w2").T.reshape(HF, P, D).transpose(1, 0, 2),
        b2=g("b2").reshape(1, D),
        router_w=a["L0_ffn_router_w"],
        moe_w1=a["L0_ffn_w1"].transpose(1, 0, 2),
        moe_w2=a["L0_ffn_w2"].reshape(NE, FE, P, D).transpose(2, 0, 1, 3),
        identity=np.eye(P, dtype=np.float32),
        select=(np.arange(BCP)[:, None] % 32 == np.arange(32)[None, :]).astype(ml_dtypes.bfloat16),
        tie_limit=np.broadcast_to(np.where(np.arange(NE)[None, :] < np.arange(NE)[:, None], np.float32(0),
                                           np.finfo(np.float32).tiny).reshape(1, NE * NE), (P, NE * NE)),
    )
    arrays = {k: np.ascontiguousarray(v) for k, v in arrays.items()}
    nc = bacc.Bacc("TRN2", target_bir_lowering=False, num_devices=1)
    args = [nc.dram_tensor(f"in_{k}", v.shape, mybir.dt.from_np(v.dtype), kind="ExternalInput").ap()
            for k, v in arrays.items()]
    out = nc.dram_tensor("out_0", (NB, T, D), FP32, kind="ExternalOutput").ap()
    mamba_moe(nc, *args, out)
    r = run_bass_kernel_spmd(nc, [{f"in_{k}": v for k, v in arrays.items()}], core_ids=[0])
    return r.results[0]["out_0"]
```
